# Optimizing a Trainium2 kernel written in Bass

```python
import numpy as np
import jax
import jax.numpy as jnp

def _softmax(x, axis=-1):
    return jax.nn.softmax(x, axis=axis)

def _gelu(x):
    return jax.nn.gelu(x, approximate=True)

def _silu(x):
    return jax.nn.silu(x)

def _sigmoid(x):
    return jax.nn.sigmoid(x)

def _layernorm(x, axis=-1, eps=1e-05):
    m = jnp.mean(x, axis=axis, keepdims=True)
    v = jnp.var(x, axis=axis, keepdims=True)
    return (x - m) / jnp.sqrt(v + eps)

def _scatter_add(tgt, idx, src, axis=0):
    return tgt.at[idx].add(src)

def _segment_sum(src, seg, n):
    return jax.ops.segment_sum(src, seg, n)
kernel_name = 'mk_gnn_preln_d2_gnn_r8_8382cb'

def setup_inputs(seed: int=0):
    np.random.seed(seed)
    _w = jnp.asarray

    def _rec_inputs():
        import jax
        import jax.numpy as jnp
        _gk = jax.random.key(seed)
        x = -0.0003713 + 1 * jax.random.normal(jax.random.fold_in(_gk, 1), (12500, 128), jnp.float32)
        _s = jax.random.randint(jax.random.fold_in(_gk, 2), (200000,), 0, 12500, jnp.int32)
        _d = jax.random.randint(jax.random.fold_in(_gk, 3), (200000,), 0, 12500, jnp.int32)
        _loop = jnp.arange(12500, dtype=jnp.int32)
        src = jnp.concatenate([_s, _d, _loop])
        dst = jnp.concatenate([_d, _s, _loop])
        _o = jnp.argsort(dst, stable=True)
        src = src[_o]
        dst = dst[_o]
        edge_attr_64 = -8.16379e-05 + 0.999858 * jax.random.normal(jax.random.fold_in(_gk, 12), (412500, 64), jnp.float32)
        edge_weight = -0.000492943 + 0.999642 * jax.random.normal(jax.random.fold_in(_gk, 14), (412500,), jnp.float32)
        return (x, src, dst, edge_attr_64, edge_weight)
    x, src, dst, edge_attr_64, edge_weight = _rec_inputs()

    def _L0_gnn_setup():
        import jax, jax.numpy as jnp
        import numpy as np
        N_NODES = 12500
        N_EDGES = 200000
        NODE_D = 128
        EDGE_D = 64
        OUT_D = 128
        key = jax.random.key(seed)
        ks = jax.random.split(key, 10)
        node_features = jax.random.normal(ks[0], (N_NODES, NODE_D), dtype=jnp.float32)
        edge_features = jax.random.normal(ks[1], (N_EDGES, EDGE_D), dtype=jnp.float32)
        src = jax.random.randint(ks[2], (N_EDGES,), 0, N_NODES, dtype=jnp.int64 if jax.config.jax_enable_x64 else jnp.int32)
        dst = jax.random.randint(ks[3], (N_EDGES,), 0, N_NODES, dtype=jnp.int64 if jax.config.jax_enable_x64 else jnp.int32)

        def lin(k, out_d, in_d):
            s = 1.0 / np.sqrt(in_d)
            kw, kb = jax.random.split(k)
            w = jax.random.uniform(kw, (out_d, in_d), minval=-s, maxval=s, dtype=jnp.float32)
            b = jax.random.uniform(kb, (out_d,), minval=-s, maxval=s, dtype=jnp.float32)
            return (w, b)
        W_msg_w, W_msg_b = lin(ks[4], OUT_D, NODE_D + EDGE_D)
        W_msg2_w, W_msg2_b = lin(ks[5], OUT_D, OUT_D)
        W_apply_w, W_apply_b = lin(ks[6], OUT_D, OUT_D + NODE_D)
        return {'node_features': node_features, 'edge_features': edge_features, 'src': src, 'dst': dst, 'W_msg_w': W_msg_w, 'W_msg_b': W_msg_b, 'W_msg2_w': W_msg2_w, 'W_msg2_b': W_msg2_b, 'W_apply_w': W_apply_w, 'W_apply_b': W_apply_b}
    _L0_gnn_all = _L0_gnn_setup()
    _L0_gnn_in = {k: v for k, v in _L0_gnn_all.items() if k in ('W_msg_w', 'W_msg_b', 'W_msg2_w', 'W_msg2_b', 'W_apply_w', 'W_apply_b')}
    del _L0_gnn_all

    def _L1_gnn_setup():
        import jax, jax.numpy as jnp
        import numpy as np
        EPS = 1e-09
        LN_EPS = 1e-05

        def _proj_normalize(v):
            return v / (jnp.linalg.norm(v, axis=-1, keepdims=True) + EPS)
        N, E, Fin, Fout = (6250, 75000, 128, 128)
        key = jax.random.key(seed)
        ks = jax.random.split(key, 8)
        x = jax.random.normal(ks[0], (N, Fin), jnp.float32)
        edge_index = jax.random.randint(ks[1], (2, E), 0, N, dtype=jnp.int64)
        edge_weight = jax.random.normal(ks[2], (E,), jnp.float32)
        W_self = jax.random.normal(ks[3], (Fin, Fout), jnp.float32) / np.sqrt(Fin)
        b_self = jnp.zeros((Fout,), jnp.float32)
        W_nb = jax.random.normal(ks[4], (Fin, Fout), jnp.float32) / np.sqrt(Fin)
        b_nb = jnp.zeros((Fout,), jnp.float32)
        gamma = jnp.ones((Fout,), jnp.float32)
        beta = jnp.zeros((Fout,), jnp.float32)
        return dict(x=x, edge_index=edge_index, edge_weight=edge_weight, W_self=W_self, b_self=b_self, W_nb=W_nb, b_nb=b_nb, gamma=gamma, beta=beta)
    _L1_gnn_all = _L1_gnn_setup()
    _L1_gnn_in = {k: v for k, v in _L1_gnn_all.items() if k in ('W_self', 'b_self', 'W_nb', 'b_nb', 'gamma', 'beta')}
    del _L1_gnn_all
    return {'x': x, 'src': src, 'dst': dst, 'edge_attr_64': edge_attr_64, 'edge_weight': edge_weight, 'L0_gnn_W_msg_w': _L0_gnn_in['W_msg_w'], 'L0_gnn_W_msg_b': _L0_gnn_in['W_msg_b'], 'L0_gnn_W_msg2_w': _L0_gnn_in['W_msg2_w'], 'L0_gnn_W_msg2_b': _L0_gnn_in['W_msg2_b'], 'L0_gnn_W_apply_w': _L0_gnn_in['W_apply_w'], 'L0_gnn_W_apply_b': _L0_gnn_in['W_apply_b'], 'L1_gnn_W_self': _L1_gnn_in['W_self'], 'L1_gnn_b_self': _L1_gnn_in['b_self'], 'L1_gnn_W_nb': _L1_gnn_in['W_nb'], 'L1_gnn_b_nb': _L1_gnn_in['b_nb'], 'L1_gnn_gamma': _L1_gnn_in['gamma'], 'L1_gnn_beta': _L1_gnn_in['beta']}

def reference(x, src, dst, edge_attr_64, edge_weight, L0_gnn_W_msg_w, L0_gnn_W_msg_b, L0_gnn_W_msg2_w, L0_gnn_W_msg2_b, L0_gnn_W_apply_w, L0_gnn_W_apply_b, L1_gnn_W_self, L1_gnn_b_self, L1_gnn_W_nb, L1_gnn_b_nb, L1_gnn_gamma, L1_gnn_beta):
    import jax
    import jax.numpy as jnp

    def _L0_gnn_ref(node_features, edge_features, src, dst, W_msg_w, W_msg_b, W_msg2_w, W_msg2_b, W_apply_w, W_apply_b):
        import jax, jax.numpy as jnp
        import numpy as np
        N_NODES = 12500
        N_EDGES = 200000
        NODE_D = 128
        EDGE_D = 64
        OUT_D = 128
        n_nodes = node_features.shape[0]
        x = jnp.concatenate([node_features[src], edge_features], axis=1)
        m = jax.nn.relu(x @ W_msg_w.T + W_msg_b)
        m = jax.nn.relu(m @ W_msg2_w.T + W_msg2_b)
        msum = jax.ops.segment_sum(m, dst, num_segments=n_nodes)
        cnt = jax.ops.segment_sum(jnp.ones((m.shape[0],), m.dtype), dst, num_segments=n_nodes)
        h_neigh = msum / jnp.maximum(cnt, 1.0)[:, None]
        out = jnp.concatenate([node_features, h_neigh], axis=1) @ W_apply_w.T + W_apply_b
        return out

    def _L1_gnn_ref(x, edge_index, edge_weight, W_self, b_self, W_nb, b_nb, gamma, beta):
        import jax, jax.numpy as jnp
        import numpy as np
        EPS = 1e-09
        LN_EPS = 1e-05

        def _proj_normalize(v):
            return v / (jnp.linalg.norm(v, axis=-1, keepdims=True) + EPS)
        N = x.shape[0]
        src, tgt = (edge_index[0], edge_index[1])
        seg_max = jax.ops.segment_max(edge_weight, tgt, num_segments=N)
        ew = jnp.exp(edge_weight - seg_max[tgt])
        denom = jax.ops.segment_sum(ew, tgt, num_segments=N)
        alpha = ew / denom[tgt]
        agg = jax.ops.segment_sum(alpha[:, None] * x[src], tgt, num_segments=N)
        agg = _proj_normalize(agg)
        self_feat = x @ W_self + b_self
        nb_feat = agg @ W_nb + b_nb
        comb = _proj_normalize(0.5 * (self_feat + nb_feat))
        mu = jnp.mean(comb, axis=-1, keepdims=True)
        var = jnp.var(comb, axis=-1, keepdims=True)
        out = (comb - mu) / jnp.sqrt(var + LN_EPS) * gamma + beta
        return out
    edge_index = jnp.stack([src, dst])
    h = jnp.maximum(_layernorm(x, axis=-1), 0.0)
    x = x + _L0_gnn_ref(h, edge_attr_64, src, dst, L0_gnn_W_msg_w, L0_gnn_W_msg_b, L0_gnn_W_msg2_w, L0_gnn_W_msg2_b, L0_gnn_W_apply_w, L0_gnn_W_apply_b)
    h = jnp.maximum(_layernorm(x, axis=-1), 0.0)
    x = x + _L1_gnn_ref(h, edge_index, edge_weight, L1_gnn_W_self, L1_gnn_b_self, L1_gnn_W_nb, L1_gnn_b_nb, L1_gnn_gamma, L1_gnn_beta)
    return x

_drawn_inputs = setup_inputs


def setup_inputs(seed=0):
    import zlib

    import numpy as np

    out = dict(_drawn_inputs(seed))
    spreads = {'L1_gnn_b_self': (0.0, 0.1),
     'L1_gnn_b_nb': (0.0, 0.1),
     'L1_gnn_gamma': (1.0, 0.2),
     'L1_gnn_beta': (0.0, 0.1)}
    factors = {'edge_attr_64': 8.0,
     'L0_gnn_W_msg_w': 4.356,
     'L0_gnn_W_msg_b': 29.882,
     'L0_gnn_W_msg2_b': 5.969,
     'edge_weight': 5.272}
    for name, (base, spread) in spreads.items():
        noise = np.random.default_rng([zlib.crc32(name.encode()), seed]).standard_normal(out[name].shape)
        drawn = base * np.exp(spread * noise) if base else spread * noise
        out[name] = jnp.asarray(drawn.astype(out[name].dtype))
    for name, factor in factors.items():
        out[name] = (out[name] * factor).astype(out[name].dtype)
    return out
```

```python
import concourse.bass as bass
from concourse import mybir
from contextlib import ExitStack

F32 = mybir.dt.float32
BF16 = mybir.dt.bfloat16
I32 = mybir.dt.int32
ALU = mybir.AluOpType
ACT = mybir.ActivationFunctionType
AX = mybir.AxisListType
ds = bass.ds

P = 128
N = 12500
E = 412500
DE = 64
G = 4
TILES_SB = 32
T = -(-E // (P * TILES_SB)) * TILES_SB
EP = T * P
NG = T // G
NBODY = NG // 8
NPOOL = T // TILES_SB
NTF, NREST = divmod(N, P)
NBATCH = -(-(N + P) // (P * G))
NT = NBATCH * G
NP = NT * P
LEN = EP // P
BIG = 3.4028234e38
LN_EPS = 1e-5
NORM_EPS = 1e-9
FILLS = -(-T // 512)
WS = ["wn", "wa1", "w2", "wa2", "wself", "wnb"]
BS = ["b_msg", "b2", "b_apply", "b_self", "b_nb", "gamma", "beta"]


def gnn(nc, x, edge_t, src_ring, dst_halo, dst_tiles, tile_base, weight_flat, mats, we, rows, out):
    p_table = nc.dram_tensor("p_table", (NP, P), F32, kind="Internal").ap()
    h_table = nc.dram_tensor("h_table", (NP, P), F32, kind="Internal").ap()
    self_rows = nc.dram_tensor("self_rows", (NP, P), F32, kind="Internal").ap()
    coef_flat = [nc.dram_tensor(n, (EP,), F32, kind="Internal").ap() for n in ("inv_flat", "alpha_flat")]

    with ExitStack() as ctx:
        def sb(name, shape, dt=F32):
            return ctx.enter_context(nc.sbuf_tensor(name, shape, dt))

        def sem(name):
            return ctx.enter_context(nc.semaphore(name))

        acc = sb("acc", [P, NP])
        xq = sb("xq", [P, NT, P])
        work = sb("work", [P, 3 * LEN])
        dloc = sb("dloc", [P, T])
        coef = sb("coef", [P, T])
        base = sb("base", [1, T], I32)
        rows_ring = sb("rows_ring", [P, 8 * G, P])
        idx = sb("idx", [P, 2, 4 * G], I32)
        onehot = sb("onehot", [P, 2, G * P])
        wmat = sb("wmat", [P, len(WS), P])
        we_sb = sb("we_sb", [P, P])
        brow = sb("brow", [P, len(BS), P])
        ident = sb("ident", [P, P])
        iota = sb("iota", [P, P])
        ones_b = sb("ones_b", [P, P], BF16)
        bias3 = sb("bias3", [P, 4, P], BF16)
        onec = sb("onec", [P, 1])
        eps = sb("eps", [P, 1])
        stat6 = sb("stat6", [P, G, 6])
        stat4 = sb("stat4", [P, G, 2])
        zeroc = sb("zeroc", [P, 1])
        stat2 = sb("stat2", [P, NT, 2])
        sc_a = sb("sc_a", [P, NT])
        sc_b = sb("sc_b", [P, NT])
        sc_c = sb("sc_c", [P, NT])
        keep = sb("keep", [P, 4])

        w = {n: wmat[:, i, :] for i, n in enumerate(WS)}
        b = {n: brow[:, i, :] for i, n in enumerate(BS)}
        bias_at = {n: i for i, n in enumerate(("b_msg", "b2", "b_apply", "b_sn"))}

        def bias_rows(n):
            return bias3[:, bias_at[n]:bias_at[n] + 1, :].to_broadcast([P, G, P])

        def four(ap):
            return ap.rearrange("p (t f) -> p t f", f=P)

        def batch(c):
            return ds(c * (G * P), G * P)

        def node_tile(c, t):
            return xq[:, ds(c * G + t, 1), :].rearrange("p a f -> p (a f)")

        def stat(arr, c, t):
            return arr[:, ds(c * G + t, 1)]

        def mean_of(c, t):
            return stat2[:, ds(c * G + t, 1), 0]

        d_halo = acc[:, 0:LEN + 2].bitcast(I32)
        lim = acc[:, 0:LEN]
        eq = acc[:, LEN + 2:2 * LEN + 3]
        wgt = acc[:, 2 * LEN + 3:3 * LEN + 3]
        fwd, tmp, tot = (work[:, n * LEN:(n + 1) * LEN] for n in range(3))
        ef_ring = work[:, 0:2048]
        z_sb = work[:, 2048:3072]
        m1t_sb = work[:, 3072:4096]
        m2_sb = work[:, 4096:5120]
        stage = four(work[:, 5120:5120 + (T // P + 1) * P])
        rowk = onehot[0:1, 0, :]
        rest, split = rows_ring[:, 20, :], rows_ring[:, 21:24, :].bitcast(BF16)[:, :, 0:P]
        normed0 = rows_ring[:, 0:4, :]
        ht0, p_out = (rows_ring[:, 4 * n:4 * n + 4, :].rearrange("p t f -> p (t f)") for n in (1, 2))
        normed1, h2_out, h2t, self_out = (work[:, 512 * n:512 * n + 512] for n in range(4))
        squares, self_in, fin, sums_in = (work[:, 512 * n:512 * n + 512] for n in range(4, 8))

        banks = [ctx.enter_context(nc.psum_tensor(f"bank{i}", [P, G * P], F32)) for i in range(8)]
        ps_z, ps_m1t, ps_m2, ps_agg = banks[0:2], banks[2:4], banks[4:6], banks[6:8]

        names = """x_loaded weights_loaded scan_inputs_loaded tile_arrays_loaded pad_zeroed constants_made
            vector_order scalar_order pool_order pool_turns vector_turns
            bias_ready var0_ready root0_ready normed0_ready normed0_turned ht0_ready pq_in_psum p_ready q_added p_stored
            ends_ready ends_turned carry_ready carry_turned less_max_ready exp_ready scalars_ready scalars_stored
            scans_done scalars_staged scalars_turned coef_filled ring_zeroed dloc_ready
            idx0_loaded_a idx0_loaded_b idx1_loaded_a idx1_loaded_b edges_loaded_a edges_loaded_b
            z_in_psum z_ready m1t_in_psum m1t_ready m2_in_psum m2_ready onehot0_ready sums0_in_psum sums0_added
            x1_sums_copied x1_in_psum x1_ready root1_ready normed1_ready h2_ready h2_stored h2_turned h2t_ready self_in_psum
            self_ready self_stored sums_zeroed
            onehot1_ready sums1_in_psum sums1_added
            squares_ready norms_in_psum norm_root_ready nb_sums_copied nb_in_psum self_loaded u_ready beta_added
            unit_arg_ready unit_root_ready var2_ready root2_ready fin_ready out_stored""".split()
        S = {n: sem(n) for n in names}
        s_rows = [[sem(f"rows{layer}_gathered_{k}") for k in range(8)] for layer in range(2)]
        s_idx = [[S["idx0_loaded_a"], S["idx0_loaded_b"]], [S["idx1_loaded_a"], S["idx1_loaded_b"]]]
        s_ef = [S["edges_loaded_a"], S["edges_loaded_b"]]

        block = ctx.enter_context(nc.Block())

        class Order:

            def __init__(self, eng, s):
                self.eng, self.s, self.start, self.n = eng, s, 0, 0

            def link(self, ins):
                self.n += 1
                ins.then_inc(self.s, 1)
                self.eng.wait_ge(self.s, self.start + self.n)

            def loop(self, count, links, body):
                start = self.start + self.n
                with self.eng.Fori(0, count) as c:
                    self.start, self.n = start + c * links, 0
                    body(c)
                    assert self.n == links, self.n
                self.start, self.n = start + count * links, 0

        def each(eng, count, body):
            body(0)
            with eng.Fori(1, count) as c:
                body(c)

        def later(c, lag=1):
            return not isinstance(c, int) or c >= lag

        def bodies(eng, body):
            each(eng, NBODY, body)
            body(NBODY)

        def live(i, k, lag):
            return not isinstance(i, int) or 0 <= 8 * i + k - lag < NG

        @block.sync
        def _(sp):
            sp.wait_ge(S["pad_zeroed"], 2)
            sp.dma_start(xq[:, 0:NTF, :], x[0:NTF * P, :].rearrange("(t p) f -> p t f", p=P)).then_inc(S["x_loaded"], 16)
            sp.dma_start(xq[0:NREST, NTF, :], x[NTF * P:N, :]).then_inc(S["x_loaded"], 16)
            sp.dma_start(wmat[:, :, :], mats.rearrange("k p f -> p k f")).then_inc(S["weights_loaded"], 16)
            sp.dma_start(we_sb[0:DE, :], we).then_inc(S["weights_loaded"], 16)
            sp.dma_start(brow[:, :, :].rearrange("p k f -> p (k f)"), rows.partition_broadcast(P)).then_inc(S["weights_loaded"], 16)
            sp.dma_start(d_halo, dst_halo).then_inc(S["scan_inputs_loaded"], 16)
            sp.dma_start(wgt, weight_flat.rearrange("(p l) -> p l", p=P)).then_inc(S["scan_inputs_loaded"], 16)
            sp.dma_start(dloc[:, :].bitcast(I32), dst_tiles).then_inc(S["tile_arrays_loaded"], 16)
            sp.dma_start(coef[:, :].bitcast(I32), tile_base.partition_broadcast(P)).then_inc(S["tile_arrays_loaded"], 16)
            sp.dma_start(base[0:1, :], tile_base.rearrange("(a t) -> a t", a=1)).then_inc(S["tile_arrays_loaded"], 16)

            def table_rows(table, c):
                return table[ds(c * (G * P), G * P), :].rearrange("(t p) f -> p t f", p=P)

            with sp.Fori(0, NBATCH) as c:
                sp.wait_ge(S["p_ready"], c + 1)
                sp.dma_start(table_rows(p_table, c), four(p_out)).then_inc(S["p_stored"], 16)

            for n in range(2):
                sp.wait_ge(S["scalars_ready"], n + 1)
                sp.dma_start(coef_flat[n].rearrange("(p l) -> p l", p=P), tot).then_inc(S["scalars_stored"], 16)

            def stage_scalars(n):
                whole = T // P
                sp.dma_start(stage[:, 0:whole, :], coef_flat[n][0:whole * P * P].rearrange("(b t e) -> t b e", t=P, e=P)).then_inc(S["scalars_staged"], 16)
                sp.dma_start(stage[0:T - whole * P, whole, :], coef_flat[n][whole * P * P:EP].rearrange("(t e) -> t e", e=P)).then_inc(S["scalars_staged"], 16)

            sp.wait_ge(S["scalars_stored"], 32)
            stage_scalars(0)

            def load_idx(layer, half, h, free):
                if free is not None:
                    sp.wait_ge(free, 4 * half - 4)
                sp.dma_start(idx[:, h, :], src_ring[ds(half, 1), :, :].rearrange("a p t -> (a p) t")).then_inc(s_idx[layer][h], 16)

            def loads0(i):
                for h in range(2):
                    half = 2 * i + h
                    load_idx(0, half, h, S["z_ready"] if later(i) else None)
                    for c in range(2):
                        chunk = 2 * half + c
                        if later(chunk, 2):
                            sp.wait_ge(S["z_in_psum"], 2 * chunk - 2)
                        sp.dma_start(ef_ring[0:DE, c * 1024:(c + 1) * 1024],
                                     edge_t[ds(chunk, 1), :, :].rearrange("a p t -> (a p) t")).then_inc(s_ef[c], 16)

            sp.wait_ge(S["ring_zeroed"], 1)
            each(sp, NPOOL, loads0)

            sp.wait_ge(S["sums0_added"], T)
            stage_scalars(1)
            for h in range(2):
                load_idx(1, h, h, None)
            with sp.Fori(0, NBATCH) as c:
                sp.wait_ge(S["h2_ready"], c + 1)
                sp.dma_start(table_rows(h_table, c), four(h2_out)).then_inc(S["h2_stored"], 16)
                sp.wait_ge(S["self_ready"], c + 1)
                sp.dma_start(table_rows(self_rows, c), four(self_out)).then_inc(S["self_stored"], 16)

            with sp.Fori(1, NPOOL) as i:
                for h in range(2):
                    load_idx(1, 2 * i + h, h, S["sums1_in_psum"])

            sp.wait_ge(S["self_stored"], 16 * NBATCH)

            def load_self(c):
                if later(c):
                    sp.wait_ge(S["u_ready"], c)
                sp.dma_start(four(self_in), table_rows(self_rows, c)).then_inc(S["self_loaded"], 16)

            each(sp, NBATCH, load_self)

            whole = NTF // G
            with sp.Fori(0, whole) as c:
                sp.wait_ge(S["fin_ready"], c + 1)
                sp.dma_start(table_rows(out, c), four(fin)).then_inc(S["out_stored"], 16)
            sp.wait_ge(S["fin_ready"], whole + 1)
            for t in range(whole * G, NTF):
                sp.dma_start(out[t * P:(t + 1) * P, :], four(fin)[:, t - whole * G, :]).then_inc(S["out_stored"], 16)
            sp.dma_start(out[NTF * P:N, :], four(fin)[0:NREST, NTF - whole * G, :]).then_inc(S["out_stored"], 16)
            sp.wait_ge(S["out_stored"], 16 * (whole + NTF - whole * G + 1))

        @block.gpsimd
        def _(pool):
            pool.memset(xq[:, NTF:NT, :], 0.0).then_inc(S["pad_zeroed"], 1)
            pool.memset(we_sb[:, :], 0.0).then_inc(S["pad_zeroed"], 1)
            pool.memset(ident[:, :], 0.0).then_inc(S["pool_order"], 1)
            pool.iota(iota[:, :], [[1, P]], base=0, channel_multiplier=0,
                      allow_small_or_imprecise_dtypes=True).then_inc(S["constants_made"], 1)
            pool.memset(ones_b[:, :], 1.0).then_inc(S["constants_made"], 1)
            pool.memset(onec[:, :], 1.0).then_inc(S["constants_made"], 1)
            pool.memset(eps[:, :], LN_EPS).then_inc(S["constants_made"], 1)
            pool.memset(zeroc[:, :], 0.0).then_inc(S["constants_made"], 1)
            pool.wait_ge(S["pool_order"], 1)
            pool.affine_select(out=ident[:, :], in_=ident[:, :], compare_op=ALU.not_equal, fill=1.0,
                               base=0, pattern=[[-1, P]], channel_multiplier=1).then_inc(S["constants_made"], 1)

            def gather(layer, table, i):
                for h in range(2):
                    pool.wait_ge(s_idx[layer][h], 16 * i + 16)
                    pool.sem_inc(S["pool_turns"], 1)
                    for k in range(4):
                        for j in range(G):
                            pool.indirect_dma_start(
                                out=rows_ring[:, 16 * h + G * k + j, :], out_offset=None, in_=table[:, :],
                                in_offset=bass.IndirectOffsetOnAxis(ap=idx[:, h, G * k + j:G * k + j + 1], axis=0),
                            ).then_inc(s_rows[layer][4 * h + k], 16)

            pool.wait_ge(S["scans_done"], 1)
            pool.wait_ge(S["scalars_stored"], 32)
            pool.memset(ef_ring[:, :], 0.0).then_inc(S["ring_zeroed"], 1)
            pool.memset(acc[:, :], 0.0).then_inc(S["ring_zeroed"], 1)
            pool.wait_ge(S["p_stored"], 16 * NBATCH)
            each(pool, NPOOL, lambda i: gather(0, p_table, i))

            with pool.Fori(0, NBATCH) as c:
                pool.wait_ge(S["x1_sums_copied"], c + 1)
                pool.sem_inc(S["pool_turns"], 1)
                pool.tensor_copy(acc[:, batch(c)], zeroc[:, :].to_broadcast([P, G * P])).then_inc(S["sums_zeroed"], 1)
            pool.wait_ge(S["h2_stored"], 16 * NBATCH)
            each(pool, NPOOL, lambda i: gather(1, h_table, i))

            with pool.Fori(0, NBATCH) as c:
                for t in range(G):
                    ins = pool.tensor_tensor(node_tile(c, t), node_tile(c, t), b["beta"], ALU.add)
                ins.then_inc(S["beta_added"], 1)

        @block.scalar
        def _(act):
            act.wait_ge(S["constants_made"], 6)
            act.wait_ge(S["var0_ready"], 1)
            act.activation(sc_a[:, :], stat2[:, :, 1], ACT.Sqrt, bias=eps[:, :]).then_inc(S["root0_ready"], 1)

            def table_p(c):
                act.wait_ge(S["normed0_turned"], c + 1)
                if later(c):
                    act.wait_ge(S["pq_in_psum"], c)
                act.activation(ht0, ps_z[0][:, :], ACT.Relu).then_inc(S["ht0_ready"], 1)
                act.wait_ge(S["pq_in_psum"], c + 1)
                if later(c):
                    act.wait_ge(S["p_stored"], 16 * c)
                act.activation(p_out, ps_m1t[0][:, :], ACT.Copy).then_inc(S["p_ready"], 1)

            each(act, NBATCH, table_p)

            act.wait_ge(S["less_max_ready"], 1)
            act.activation(wgt, wgt, ACT.Exp).then_inc(S["exp_ready"], 1)

            def fill(n):
                for q in range(FILLS):
                    act.wait_ge(S["scalars_turned"], n * FILLS + q + 1)
                    width = min(512, T - 512 * q)
                    act.activation(coef[:, 512 * q:512 * q + width], ps_m1t[q % 2][:, 0:width], ACT.Copy).then_inc(S["coef_filled"], 1)

            act.wait_ge(S["dloc_ready"], 1)
            fill(0)

            def layer0(i):
                for k in range(8):
                    if live(i, k, 1):
                        g, slot = 8 * i + k - 1, (k + 1) % 2
                        act.wait_ge(S["m1t_in_psum"], g + 1)
                        if later(g, 2):
                            act.wait_ge(S["m2_in_psum"], g - 1)
                        act.activation(m1t_sb[:, 512 * slot:512 * slot + 512], ps_m1t[slot][:, :], ACT.Relu).then_inc(S["m1t_ready"], 1)
                    if live(i, k, 2):
                        g, slot = 8 * i + k - 2, k % 2
                        act.wait_ge(S["m2_in_psum"], g + 1)
                        if later(g, 2):
                            act.wait_ge(S["sums0_in_psum"], g - 1)
                        act.activation(m2_sb[:, 512 * slot:512 * slot + 512], ps_m2[slot][:, :], ACT.Relu).then_inc(S["m2_ready"], 1)

            bodies(act, layer0)

            act.wait_ge(S["sums0_added"], T)
            fill(1)

            def copy_sums(copied, used):
                def body(c):
                    if later(c):
                        act.wait_ge(used, c)
                    act.activation(sums_in, acc[:, batch(c)], ACT.Copy).then_inc(copied, 1)
                each(act, NBATCH, body)

            copy_sums(S["x1_sums_copied"], S["x1_in_psum"])
            act.wait_ge(S["x1_ready"], NBATCH)
            act.activation(sc_a[:, :], stat2[:, :, 1], ACT.Sqrt, bias=eps[:, :]).then_inc(S["root1_ready"], 1)

            def middle(c):
                act.wait_ge(S["normed1_ready"], c + 1)
                if later(c):
                    act.wait_ge(S["h2_stored"], 16 * c)
                    act.wait_ge(S["h2_turned"], c)
                act.activation(h2_out, normed1, ACT.Relu).then_inc(S["h2_ready"], 1)
                act.wait_ge(S["h2_turned"], c + 1)
                if later(c):
                    act.wait_ge(S["self_in_psum"], c)
                act.activation(h2t, ps_m1t[0][:, :], ACT.Copy).then_inc(S["h2t_ready"], 1)
                act.wait_ge(S["self_in_psum"], c + 1)
                if later(c):
                    act.wait_ge(S["self_stored"], 16 * c)
                act.activation(self_out, ps_m2[0][:, :], ACT.Copy).then_inc(S["self_ready"], 1)

            each(act, NBATCH, middle)

            act.wait_ge(S["sums1_added"], T)

            def norms(c):
                if later(c):
                    act.wait_ge(S["norms_in_psum"], c)
                act.activation(squares, acc[:, batch(c)], ACT.Square).then_inc(S["squares_ready"], 1)

            each(act, NBATCH, norms)
            act.wait_ge(S["norms_in_psum"], NBATCH)
            act.activation(sc_a[:, :], ps_z[0][:, 0:NT], ACT.Sqrt).then_inc(S["norm_root_ready"], 1)
            copy_sums(S["nb_sums_copied"], S["nb_in_psum"])
            act.wait_ge(S["unit_arg_ready"], 1)
            act.activation(sc_b[:, :], sc_b[:, :], ACT.Sqrt).then_inc(S["unit_root_ready"], 1)
            act.wait_ge(S["var2_ready"], 1)
            act.activation(sc_c[:, :], sc_c[:, :], ACT.Sqrt, bias=eps[:, :]).then_inc(S["root2_ready"], 1)

        @block.vector
        def _(dve):
            order = Order(dve, S["vector_order"])
            link = order.link

            def statistics(src, c):
                dve.sem_inc(S["vector_turns"], 1)
                for t in range(G):
                    ins = dve.bn_stats(stat6[:, t, :], src(c, t))
                link(ins)
                dve.sem_inc(S["vector_turns"], 1)
                for t in range(G):
                    ins = dve.bn_aggr(stat4[:, t, :], stat6[:, t, :])
                link(ins)
                link(dve.tensor_copy(stat2[:, ds(c * G, G), :], stat4[:, :, :]))

            def normalise(dst, src, c, scale):
                for t in range(G):
                    ins = dve.tensor_scalar(dst[:, t, :], src(c, t), mean_of(c, t), stat(scale, c, t), ALU.subtract, ALU.mult)
                return ins

            dve.wait_ge(S["x_loaded"], 32)
            order.loop(NBATCH, 3, lambda c: statistics(node_tile, c))
            link(dve.memset(rowk[:, :], 0.0))
            dve.sem_inc(S["var0_ready"], 1)
            dve.wait_ge(S["weights_loaded"], 48)
            dve.wait_ge(S["constants_made"], 6)
            link(dve.tensor_tensor(b["b_self"], b["b_self"], b["b_nb"], ALU.add))
            for n, at in (("b_msg", 0), ("b2", 1), ("b_apply", 2), ("b_self", 3)):
                link(dve.tensor_copy(split[:, 0, :], b[n]))
                link(dve.tensor_tensor(rest, b[n], split[:, 0, :], ALU.subtract))
                link(dve.tensor_copy(split[:, 1, :], rest))
                link(dve.tensor_tensor(rest, rest, split[:, 1, :], ALU.subtract))
                link(dve.tensor_copy(split[:, 2, :], rest))
                link(dve.tensor_scalar(bias3[:, at, :], split[:, 0, :], ident[:, 0:1], None, ALU.mult))
                for part in (1, 2):
                    link(dve.scalar_tensor_tensor(bias3[:, at, :], split[:, part, :], ident[:, part:part + 1], bias3[:, at, :], ALU.mult, ALU.add))
            dve.sem_inc(S["bias_ready"], 1)
            dve.wait_ge(S["root0_ready"], 1)
            link(dve.reciprocal(sc_a[:, :], sc_a[:, :]))

            def norm0(c):
                if later(c):
                    dve.wait_ge(S["normed0_turned"], c)
                normalise(normed0, node_tile, c, sc_a).then_inc(S["normed0_ready"], 1)

            def add_q(c):
                dve.wait_ge(S["pq_in_psum"], c + 1)
                q = xq[:, ds(c * G, G), :]
                dve.tensor_tensor(q, q, four(ps_m1t[1][:, :]), ALU.add).then_inc(S["q_added"], 1)

            norm0(0)
            with dve.Fori(1, NBATCH) as c:
                norm0(c)
                add_q(c - 1)
            add_q(NBATCH - 1)

            dve.wait_ge(S["tile_arrays_loaded"], 48)
            dve.tensor_tensor(dloc[:, :], dloc[:, :].bitcast(I32), coef[:, :].bitcast(I32), ALU.subtract).then_inc(S["dloc_ready"], 1)

            dve.wait_ge(S["scan_inputs_loaded"], 32)
            link(dve.tensor_tensor(eq, d_halo[:, 1:LEN + 2], d_halo[:, 0:LEN + 1], ALU.is_equal))
            link(dve.tensor_reduce(keep[:, 0:1], eq[:, 0:LEN], AX.X, ALU.min))
            link(dve.tensor_reduce(keep[:, 1:2], eq[:, 1:LEN + 1], AX.X, ALU.min))
            same_before, same_after = eq[:, 0:LEN], eq[:, 1:LEN + 1]
            carries = [0]

            def scan(dst, mask, data, op0, op1, initial, back):
                way = slice(None, None, -1) if back else slice(None)
                link(dve.tensor_tensor_scan(dst[:, way], mask[:, way], data[:, way], initial, op0, op1))

            def carried_scan(dst, mask, data, op0, op1, initial, back):
                scan(dst, mask, data, op0, op1, initial, back)
                carries[0] += 1
                n = carries[0]
                end = dst[:, 0:1] if back else dst[:, LEN - 1:LEN]
                link(dve.tensor_copy(keep[:, 2:3], end))
                dve.sem_inc(S["ends_ready"], 1)
                dve.wait_ge(S["ends_turned"], n)
                link(dve.tensor_copy(rowk[0:1, 0:2 * P], ps_z[0][0:1, 0:2 * P]))
                ends, flags = rowk[0:1, 0:P], rowk[0:1, P:2 * P]
                if op0 == ALU.min:
                    link(dve.tensor_scalar(flags, flags, 2.0, -1.0, ALU.mult, ALU.add))
                    link(dve.tensor_scalar(flags, flags, BIG, None, ALU.mult))
                if back:
                    link(dve.tensor_tensor_scan(rowk[0:1, 3 * P:4 * P - 1][:, ::-1], flags[:, 1:P][:, ::-1], ends[:, 1:P][:, ::-1], initial, op0, op1))
                else:
                    link(dve.tensor_tensor_scan(rowk[0:1, 2 * P + 1:3 * P], flags[:, 0:P - 1], ends[:, 0:P - 1], initial, op0, op1))
                dve.sem_inc(S["carry_ready"], 1)
                dve.wait_ge(S["carry_turned"], n)
                link(dve.tensor_copy(keep[:, 3:4], ps_z[1][:, 0:1]))
                scan(dst, mask, data, op0, op1, keep[:, 3:4], back)

            def over_segment(mask, data, op0, op1, initial):
                carried_scan(fwd, mask, data, op0, op1, initial, False)
                link(dve.scalar_tensor_tensor(tmp, same_after, 0.0, fwd, ALU.is_equal, ALU.mult))
                carried_scan(tot, same_after, tmp, ALU.mult, ALU.add, 0.0, True)

            link(dve.memset(lim, 1.0))
            over_segment(same_before, lim, ALU.mult, ALU.add, 0.0)
            dve.reciprocal(tot, tot).then_inc(S["scalars_ready"], 1)
            link(dve.tensor_scalar(lim, same_before, 2.0, -1.0, ALU.mult, ALU.add))
            link(dve.tensor_scalar(lim, lim, BIG, None, ALU.mult))
            dve.wait_ge(S["scalars_stored"], 16)
            over_segment(lim, wgt, ALU.min, ALU.max, -BIG)
            dve.tensor_tensor(wgt, wgt, tot, ALU.subtract).then_inc(S["less_max_ready"], 1)
            dve.wait_ge(S["exp_ready"], 1)
            over_segment(same_before, wgt, ALU.mult, ALU.add, 0.0)
            link(dve.reciprocal(tot, tot))
            dve.tensor_tensor(tot, tot, wgt, ALU.mult).then_inc(S["scalars_ready"], 1)
            dve.sem_inc(S["scans_done"], 1)

            def bases(group):
                _, at = nc.values_load_multi_w_load_instructions(
                    base[0:1, ds(G * group, G)], engines=[mybir.EngineType.DVE], min_val=0, max_val=N,
                    skip_runtime_bounds_check_because="destinations are nodes or N")
                return at

            def sums_and_onehots(i, k, lag_sum, lag_hot, in_psum, added, hot):
                adds, hots = live(i, k, lag_sum), live(i, k, lag_hot)
                gs, gh = 8 * i + k - lag_sum, 8 * i + k - lag_hot
                if adds:
                    at = bases(gs)
                    dve.wait_ge(in_psum, gs + 1)
                for j in range(G):
                    if adds:
                        if later(gs * G + j):
                            dve.wait_ge(added, gs * G + j)
                        win = acc[:, ds(at[j], P)]
                        dve.tensor_tensor(win, win, ps_agg[k % 2][:, j * P:(j + 1) * P], ALU.add).then_inc(added, 1)
                    if hots:
                        t = gh * G + j
                        ins = dve.tensor_scalar(onehot[:, k % 2, j * P:(j + 1) * P], iota[:, :], dloc[:, ds(t, 1)], coef[:, ds(t, 1)],
                                                ALU.is_equal, ALU.mult)
                if hots:
                    ins.then_inc(hot, 1)

            def layer0(i):
                for k in range(8):
                    g, slot = 8 * i + k, k % 2
                    if live(i, k, 0):
                        dve.wait_ge(S["z_in_psum"], g + 1)
                        dve.wait_ge(s_rows[0][k], 64 * i + 64)
                        if later(g, 2):
                            dve.wait_ge(S["m1t_in_psum"], g - 1)
                        dve.tensor_tensor(four(z_sb[:, 512 * slot:512 * slot + 512]), four(ps_z[slot][:, :]),
                                          rows_ring[:, G * k:G * k + G, :], ALU.add).then_inc(S["z_ready"], 1)
                    sums_and_onehots(i, k, 4, 2, S["sums0_in_psum"], S["sums0_added"], S["onehot0_ready"])

            dve.wait_ge(S["coef_filled"], FILLS)
            dve.wait_ge(S["ring_zeroed"], 2)
            bodies(dve, layer0)

            def x1(c):
                dve.wait_ge(S["x1_in_psum"], c + 1)
                q = xq[:, ds(c * G, G), :]
                link(dve.tensor_tensor(q, q, four(ps_z[0][:, :]), ALU.add))
                statistics(node_tile, c)
                dve.sem_inc(S["x1_ready"], 1)

            order.loop(NBATCH, 4, x1)
            dve.wait_ge(S["root1_ready"], 1)
            link(dve.reciprocal(sc_a[:, :], sc_a[:, :]))

            def norm1(c):
                if later(c):
                    dve.wait_ge(S["h2_ready"], c)
                normalise(four(normed1), node_tile, c, sc_a).then_inc(S["normed1_ready"], 1)

            each(dve, NBATCH, norm1)

            dve.wait_ge(S["coef_filled"], 2 * FILLS)
            dve.wait_ge(S["sums_zeroed"], NBATCH)
            bodies(dve, lambda i: [sums_and_onehots(i, k, 2, 0, S["sums1_in_psum"], S["sums1_added"], S["onehot1_ready"]) for k in range(8)])

            dve.wait_ge(S["norm_root_ready"], 1)
            link(dve.tensor_scalar(sc_a[:, :], sc_a[:, :], NORM_EPS, None, ALU.add))
            link(dve.reciprocal(sc_a[:, :], sc_a[:, :]))

            def u_tile(c, t):
                return acc[:, ds(c * (G * P) + t * P, P)]

            def u_rows(c):
                dve.wait_ge(S["nb_in_psum"], c + 1)
                dve.wait_ge(S["self_loaded"], 16 * c + 16)
                for t in range(G):
                    ins = dve.scalar_tensor_tensor(u_tile(c, t), ps_m1t[0][:, t * P:(t + 1) * P], stat(sc_a, c, t),
                                                   four(self_in)[:, t, :], ALU.mult, ALU.add)
                link(ins)
                dve.sem_inc(S["u_ready"], 1)
                statistics(u_tile, c)

            order.loop(NBATCH, 4, u_rows)
            mean, var = stat2[:, :, 0], stat2[:, :, 1]
            link(dve.tensor_tensor(sc_b[:, :], mean, mean, ALU.mult))
            link(dve.tensor_tensor(sc_b[:, :], sc_b[:, :], var, ALU.add))
            dve.tensor_scalar(sc_b[:, :], sc_b[:, :], P / 4.0, None, ALU.mult).then_inc(S["unit_arg_ready"], 1)
            dve.wait_ge(S["unit_root_ready"], 1)
            link(dve.tensor_scalar(sc_b[:, :], sc_b[:, :], NORM_EPS, None, ALU.add))
            link(dve.reciprocal(sc_b[:, :], sc_b[:, :]))
            link(dve.tensor_scalar(sc_b[:, :], sc_b[:, :], 0.5, None, ALU.mult))
            link(dve.tensor_tensor(sc_c[:, :], sc_b[:, :], sc_b[:, :], ALU.mult))
            dve.tensor_tensor(sc_c[:, :], sc_c[:, :], var, ALU.mult).then_inc(S["var2_ready"], 1)
            dve.wait_ge(S["root2_ready"], 1)
            link(dve.reciprocal(sc_c[:, :], sc_c[:, :]))
            link(dve.tensor_tensor(sc_c[:, :], sc_c[:, :], sc_b[:, :], ALU.mult))
            gamma4 = brow[:, BS.index("gamma"):BS.index("gamma") + 1, :].to_broadcast([P, G, P])

            start = order.start + order.n

            def last(c):
                order.start, order.n = start + 2 * c, 0
                u4 = four(acc[:, batch(c)])
                for t in range(G):
                    ins = dve.tensor_scalar(u_tile(c, t), u_tile(c, t), mean_of(c, t), stat(sc_c, c, t), ALU.subtract, ALU.mult)
                link(ins)
                link(dve.tensor_tensor(u4, u4, gamma4, ALU.mult))
                dve.wait_ge(S["beta_added"], c + 1)
                if later(c):
                    dve.wait_ge(S["out_stored"], 16 * c)
                dve.tensor_tensor(four(fin), u4, xq[:, ds(c * G, G), :], ALU.add).then_inc(S["fin_ready"], 1)

            each(dve, NBATCH, last)

        @block.tensor
        def _(pe):
            def tiles(ap):
                return [ap[:, t * P:(t + 1) * P] for t in range(G)]

            def turn(dst, src):
                for d, s in zip(tiles(dst), src):
                    ins = pe.transpose(d, s, ident[:, :])
                return ins

            def products(dst, left, right, bias=None):
                if bias is not None:
                    pe.matmul(four(dst), ones_b[:, :], bias_rows(bias), start=True, stop=False)
                for t, (d, l) in enumerate(zip(tiles(dst), left)):
                    ins = pe.matmul(d, l, right[t] if isinstance(right, list) else right,
                                    start=bias is None, stop=bias is None or t == G - 1)
                return ins

            pe.wait_ge(S["constants_made"], 6)
            pe.wait_ge(S["weights_loaded"], 48)
            pe.wait_ge(S["bias_ready"], 1)

            def table_p(c):
                pe.wait_ge(S["normed0_ready"], c + 1)
                if later(c):
                    pe.wait_ge(S["ht0_ready"], c)
                turn(ps_z[0][:, :], [normed0[:, t, :] for t in range(G)]).then_inc(S["normed0_turned"], 1)
                pe.wait_ge(S["ht0_ready"], c + 1)
                if later(c):
                    pe.wait_ge(S["p_ready"], c)
                    pe.wait_ge(S["q_added"], c)
                products(ps_m1t[0][:, :], tiles(ht0), w["wn"], "b_msg")
                products(ps_m1t[1][:, :], tiles(ht0), w["wa1"], "b_apply").then_inc(S["pq_in_psum"], 1)

            each(pe, NBATCH, table_p)

            for n in range(6):
                back = n % 2
                pe.wait_ge(S["ends_ready"], n + 1)
                pe.matmul(ps_z[0][0:1, 0:P], keep[:, 2:3], ident[:, :], start=True, stop=True)
                pe.matmul(ps_z[0][0:1, P:2 * P], keep[:, back:back + 1], ident[:, :], start=True, stop=True).then_inc(S["ends_turned"], 1)
                pe.wait_ge(S["carry_ready"], n + 1)
                at = (3 if back else 2) * P
                pe.matmul(ps_z[1][:, 0:1], rowk[0:1, at:at + P], onec[0:1, 0:1], start=True, stop=True).then_inc(S["carry_turned"], 1)

            def fill(n):
                pe.wait_ge(S["scalars_staged"], 32 * n + 32)
                for q in range(FILLS):
                    if later(n * FILLS + q, 2):
                        pe.wait_ge(S["coef_filled"], n * FILLS + q - 1) if n * FILLS + q > 1 else None
                    for j in range(4 * q, min(4 * q + 4, T // P + 1)):
                        h = min(P, T - j * P)
                        ins = pe.transpose(ps_m1t[q % 2][:, (j % 4) * P:(j % 4) * P + h], stage[0:h, j, :], ident[0:h, 0:h])
                    ins.then_inc(S["scalars_turned"], 1)

            fill(0)
            pe.wait_ge(S["ring_zeroed"], 2)

            def layer0(i):
                for k in range(8):
                    if live(i, k, 0):
                        g, slot, c = 8 * i + k, k % 2, k // 2 % 2
                        pe.wait_ge(s_ef[c], 32 * i + 16 * (k // 4) + 16)
                        if later(g, 2):
                            pe.wait_ge(S["z_ready"], g - 1)
                        at = c * 1024 + slot * 512
                        products(ps_z[slot][:, :], tiles(ef_ring[:, at:at + 512]), we_sb[:, :]).then_inc(S["z_in_psum"], 1)
                    if live(i, k, 1):
                        g, slot = 8 * i + k - 1, (k + 1) % 2
                        pe.wait_ge(S["z_ready"], g + 1)
                        if later(g, 2):
                            pe.wait_ge(S["m1t_ready"], g - 1)
                        turn(ps_m1t[slot][:, :], tiles(z_sb[:, 512 * slot:512 * slot + 512])).then_inc(S["m1t_in_psum"], 1)
                    if live(i, k, 2):
                        g, slot = 8 * i + k - 2, k % 2
                        pe.wait_ge(S["m1t_ready"], g + 1)
                        if later(g, 2):
                            pe.wait_ge(S["m2_ready"], g - 1)
                        products(ps_m2[slot][:, :], tiles(m1t_sb[:, 512 * slot:512 * slot + 512]), w["w2"], "b2").then_inc(S["m2_in_psum"], 1)
                    if live(i, k, 3):
                        g, slot = 8 * i + k - 3, (k + 1) % 2
                        pe.wait_ge(S["m2_ready"], g + 1)
                        pe.wait_ge(S["onehot0_ready"], g + 1)
                        if later(g, 2):
                            pe.wait_ge(S["sums0_added"], 4 * g - 4)
                        products(ps_agg[slot][:, :], tiles(m2_sb[:, 512 * slot:512 * slot + 512]),
                                 tiles(onehot[:, slot, :])).then_inc(S["sums0_in_psum"], 1)

            bodies(pe, layer0)

            pe.wait_ge(S["sums0_added"], T)
            fill(1)

            def x1(c):
                if later(c):
                    pe.wait_ge(S["x1_ready"], c)
                pe.wait_ge(S["x1_sums_copied"], c + 1)
                products(ps_z[0][:, :], tiles(sums_in), w["wa2"]).then_inc(S["x1_in_psum"], 1)

            each(pe, NBATCH, x1)

            def self_part(c):
                pe.wait_ge(S["h2_ready"], c + 1)
                if later(c):
                    pe.wait_ge(S["h2t_ready"], c)
                else:
                    pe.wait_ge(S["coef_filled"], 2 * FILLS)
                turn(ps_m1t[0][:, :], tiles(h2_out)).then_inc(S["h2_turned"], 1)
                pe.wait_ge(S["h2t_ready"], c + 1)
                if later(c):
                    pe.wait_ge(S["self_ready"], c)
                products(ps_m2[0][:, :], tiles(h2t), w["wself"], "b_sn").then_inc(S["self_in_psum"], 1)

            each(pe, NBATCH, self_part)

            def layer1(i):
                for k in range(8):
                    if live(i, k, 0):
                        g, slot = 8 * i + k, k % 2
                        pe.wait_ge(s_rows[1][k], 64 * i + 64)
                        pe.wait_ge(S["onehot1_ready"], g + 1)
                        if later(g, 2):
                            pe.wait_ge(S["sums1_added"], 4 * g - 4)
                        products(ps_agg[slot][:, :], [rows_ring[:, G * k + j, :] for j in range(G)],
                                 tiles(onehot[:, slot, :])).then_inc(S["sums1_in_psum"], 1)

            each(pe, NBODY, layer1)

            def norms(c):
                pe.wait_ge(S["squares_ready"], c + 1)
                for t in range(G):
                    ins = pe.matmul(ps_z[0][:, ds(c * G + t, 1)], squares[:, t * P:(t + 1) * P], onec[:, :], start=True, stop=True)
                ins.then_inc(S["norms_in_psum"], 1)

            each(pe, NBATCH, norms)

            def neighbours(c):
                if later(c):
                    pe.wait_ge(S["u_ready"], c)
                pe.wait_ge(S["nb_sums_copied"], c + 1)
                products(ps_m1t[0][:, :], tiles(sums_in), w["wnb"]).then_inc(S["nb_in_psum"], 1)

            each(pe, NBATCH, neighbours)


_ARGS = ["x", "edge_t", "src_ring", "dst_halo", "dst_tiles", "tile_base", "weight_flat", "mats", "we", "rows"]


def kernel(x, src, dst, edge_attr_64, edge_weight, L0_gnn_W_msg_w, L0_gnn_W_msg_b, L0_gnn_W_msg2_w, L0_gnn_W_msg2_b,
           L0_gnn_W_apply_w, L0_gnn_W_apply_b, L1_gnn_W_self, L1_gnn_b_self, L1_gnn_W_nb, L1_gnn_b_nb, L1_gnn_gamma,
           L1_gnn_beta):
    import numpy as np
    import concourse.bacc as bacc
    from concourse.bass_utils import run_bass_kernel_spmd as run

    c = np.ascontiguousarray
    pad = EP - E
    dst_pad = np.pad(np.asarray(dst), (0, pad), constant_values=N)
    src_pad = np.pad(np.asarray(src), (0, pad))
    ends = np.pad(dst_pad, 1, constant_values=-1)
    edges = np.pad(np.asarray(edge_attr_64), ((0, pad), (0, 0)))
    wm, wa = np.asarray(L0_gnn_W_msg_w), np.asarray(L0_gnn_W_apply_w)
    arrays = {
        "x": c(x),
        "edge_t": c(edges.reshape(EP // 1024, 1024, DE).transpose(0, 2, 1)),
        "src_ring": c(src_pad.reshape(T // 16, 16, P).transpose(0, 2, 1)),
        "dst_halo": np.stack([ends[p * LEN:p * LEN + LEN + 2] for p in range(P)]),
        "dst_tiles": c(dst_pad.reshape(T, P).T),
        "tile_base": c(dst_pad.reshape(T, P)[:, 0]),
        "weight_flat": np.pad(np.asarray(edge_weight), (0, pad)),
        "mats": np.stack([wm[:, :P].T, wa[:, :P].T, np.asarray(L0_gnn_W_msg2_w).T, wa[:, P:].T,
                          np.asarray(L1_gnn_W_self), np.asarray(L1_gnn_W_nb)]),
        "we": c(wm[:, P:].T),
        "rows": np.concatenate([np.asarray(v) for v in (L0_gnn_W_msg_b, L0_gnn_W_msg2_b, L0_gnn_W_apply_b, L1_gnn_b_self,
                                                        L1_gnn_b_nb, L1_gnn_gamma, L1_gnn_beta)]),
    }
    nc = bacc.Bacc("TRN2", target_bir_lowering=False, num_devices=1)
    ins = [nc.dram_tensor(f"in_{n}", arrays[n].shape, mybir.dt.from_np(arrays[n].dtype), kind="ExternalInput").ap() for n in _ARGS]
    out = nc.dram_tensor("rows_out", (N, P), F32, kind="ExternalOutput").ap()
    gnn(nc, *ins, out)
    r = run(nc, [{f"in_{n}": arrays[n] for n in _ARGS}], core_ids=[0])
    return r.results[0]["rows_out"]
```

```python
import concourse.bass as bass
from concourse import mybir
from contextlib import ExitStack

F32 = mybir.dt.float32
BF16 = mybir.dt.bfloat16
I32 = mybir.dt.int32
ALU = mybir.AluOpType
ACT = mybir.ActivationFunctionType
AX = mybir.AxisListType
ds = bass.ds

P = 128
N = 12500
E = 412500
DE = 64
G = 4
TILES_SB = 32
T = -(-E // (P * TILES_SB)) * TILES_SB
EP = T * P
NG = T // G
NBODY = NG // 8
NPOOL = T // TILES_SB
NTF, NREST = divmod(N, P)
NBATCH = -(-(N + P) // (P * G))
NT = NBATCH * G
NP = NT * P
LEN = EP // P
BIG = 3.4028234e38
LN_EPS = 1e-5
NORM_EPS = 1e-9
FILLS = -(-T // 512)
WS = ["wn", "wa1", "w2", "wa2", "wself", "wnb"]
BS = ["b_msg", "b2", "b_apply", "b_self", "b_nb", "gamma", "beta"]


def gnn(nc, x, edge_t, src_ring, dst_halo, dst_tiles, tile_base, weight_flat, mats, we, rows, out):
    p_table = nc.dram_tensor("p_table", (NP, P), F32, kind="Internal").ap()
    h_table = nc.dram_tensor("h_table", (NP, P), F32, kind="Internal").ap()
    ht_rows = nc.dram_tensor("ht_rows", (NBATCH * P, G * P), F32, kind="Internal").ap()
    self_rows = nc.dram_tensor("self_rows", (NP, P), F32, kind="Internal").ap()
    coef_flat = [nc.dram_tensor(n, (EP,), F32, kind="Internal").ap() for n in ("inv_flat", "alpha_flat")]

    with ExitStack() as ctx:
        def sb(name, shape, dt=F32):
            return ctx.enter_context(nc.sbuf_tensor(name, shape, dt))

        def sem(name):
            return ctx.enter_context(nc.semaphore(name))

        acc = sb("acc", [P, NP])
        xq = sb("xq", [P, NT, P])
        work = sb("work", [P, (10 * G + T // P + 1) * P])
        dloc = sb("dloc", [P, T])
        coef = sb("coef", [P, T])
        base = sb("base", [1, T], I32)
        rows_ring = sb("rows_ring", [P, 8 * G, P])
        idx = sb("idx", [P, 2, 4 * G], I32)
        onehot = sb("onehot", [P, 2, G * P])
        wmat = sb("wmat", [P, len(WS), P])
        we_sb = sb("we_sb", [P, P])
        brow = sb("brow", [P, len(BS), P])
        ident = sb("ident", [P, P])
        iota = sb("iota", [P, P])
        ones_b = sb("ones_b", [P, P], BF16)
        bias3 = sb("bias3", [P, 4, P], BF16)
        onec = sb("onec", [P, 1])
        zeroc = sb("zeroc", [P, 1])
        eps = sb("eps", [P, 1])
        stat6 = sb("stat6", [P, NT, 6])
        mean = sb("mean", [P, NT])
        var = sb("var", [P, NT])
        sc_a = sb("sc_a", [P, NT])
        sc_b = sb("sc_b", [P, NT])
        keep = sb("keep", [P, 4])
        rowk = sb("rowk", [1, 4 * P])

        w = {n: wmat[:, i, :] for i, n in enumerate(WS)}
        b = {n: brow[:, i, :] for i, n in enumerate(BS)}
        bias_at = {n: i for i, n in enumerate(("b_msg", "b2", "b_apply", "b_sn"))}

        def bias_rows(n):
            return bias3[:, bias_at[n]:bias_at[n] + 1, :].to_broadcast([P, G, P])

        def over4(n):
            return brow[:, BS.index(n):BS.index(n) + 1, :].to_broadcast([P, G, P])

        def four(ap):
            return ap.rearrange("p (t f) -> p t f", f=P)

        def flat(ap):
            return ap.rearrange("p t f -> p (t f)")

        def tiles(ap):
            return [ap[:, t * P:(t + 1) * P] for t in range(G)]

        def batch(c):
            return ds(c * (G * P), G * P)

        def q_rows(c):
            return xq[:, ds(c * G, G), :]

        def q_tile(c, t):
            return flat(xq[:, ds(c * G + t, 1), :])

        def u_tile(c, t):
            return acc[:, ds(c * (G * P) + t * P, P)]

        def of_tile(arr, c, t):
            return arr[:, ds(c * G + t, 1)]

        def scan_arrays(room):
            halo = room[:, 0:LEN + 2].bitcast(I32)
            eq = room[:, 3 * LEN + 2:3 * LEN + 2 + (LEN + 2) // 2].bitcast(BF16)[:, 0:LEN + 1]
            return halo, room[:, 0:LEN], room[:, LEN + 2:2 * LEN + 2], room[:, 2 * LEN + 2:3 * LEN + 2], eq

        cnt_arrays = scan_arrays(acc)
        soft_arrays = scan_arrays(flat(xq[:, :, :]))
        place = [work[:, 512 * n:512 * n + 512] for n in range(10)]
        stage = four(work[:, 10 * 512:])
        wgt = work[:, 10 * 512:10 * 512 + LEN]
        ef_ring, z_sb, m1t_sb, m2_sb = work[:, 0:2048], place[4:6], place[6:8], place[8:10]
        ring4 = [rows_ring[:, 4 * n:4 * n + 4, :] for n in range(6)]
        normed0, ht0, p_out = ring4[0:2], [flat(r) for r in ring4[2:4]], [flat(r) for r in ring4[4:6]]
        rest, split = flat(rows_ring[:, 24:28, :]), flat(rows_ring[:, 28:30, :]).bitcast(BF16)
        ht_in, sums_in, normed1, h2_out = place[0:2] + place[4:6], place[2:4], place[4:6], place[6:10]
        h2_in, h2t, self_out = place[8:10], place[0:2], place[4:6]
        squares, self_in, fin = place[6:8] + place[2:4], place[4:6] + place[8:10], place[0:2]

        banks = [ctx.enter_context(nc.psum_tensor(f"bank{i}", [P, G * P], F32)) for i in range(8)]
        ps_z, ps_m1t, ps_m2, ps_agg = banks[0:2], banks[2:4], banks[4:6], banks[6:8]
        ps_nb = banks[2:6]

        names = """weights_loaded counts_in_loaded soft_in_loaded tile_arrays_loaded pad_zeroed constants_made
            vector_order pool_order pool_turns vector_turns
            bias_ready var0_ready root0_ready normed0_ready normed0_turned ht0_ready p_in_psum p_ready
            ends_ready ends_turned ends_read carry_ready carry_turned carry_read
            less_max_ready exp_ready scalars_ready scalars_stored
            scalars_staged scalars_turned coef_filled sums_zeroed0 ring_zeroed dloc_ready x_reloaded
            counts_made z_in_psum z_ready m1t_in_psum m1t_ready m2_in_psum m2_ready onehot0_ready sums0_in_psum sums0_added
            x1_sums_copied x1_in_psum x1_added var1_ready root1_ready normed1_ready h2_ready sums_zeroed1
            h2_turned h2t_ready self_in_psum self_ready
            onehot1_ready sums1_in_psum sums1_added
            squares_ready norms_in_psum norm_root_ready nb_sums_copied nb_in_psum u_ready
            unit_arg_ready unit_root_ready var2_ready root2_ready centred_ready scaled_ready fin_ready""".split()
        S = {n: sem(n) for n in names}
        pair_names = "ht_stored p_stored h2_loaded self_stored out_stored edges_loaded idx0_loaded idx1_loaded"
        S2 = {n: [sem(f"{n}_{h}") for h in range(2)] for n in pair_names.split()}
        S2 |= {n: [sem(f"{n}_{h}") for h in range(4)] for n in ("ht_loaded", "h2_stored", "self_loaded")}
        s_x = [sem(f"x_loaded_{n}") for n in range(4)]
        s_rows = [[sem(f"rows{layer}_gathered_{k}") for k in range(8)] for layer in range(2)]
        s_idx = [S2["idx0_loaded"], S2["idx1_loaded"]]

        block = ctx.enter_context(nc.Block())

        def later(c, lag=1):
            return not isinstance(c, int) or c >= lag

        def each(eng, count, body):
            body(0)
            with eng.Fori(1, count) as c:
                body(c)

        def rounds(eng, body, slots, lag=0):
            for c in range(slots):
                body(c, c, 0)
            with eng.Fori(1, NBATCH // slots) as i:
                for h in range(slots):
                    body(slots * i + h, h, i)
            for c in range(NBATCH // slots * slots, NBATCH + lag):
                body(c, c % slots, c // slots)

        def pairs(eng, body, lag=0):
            rounds(eng, body, 2, lag)

        def used(slots, h):
            return (NBATCH - 1 - h) // slots + 1

        def has(c, lag=0):
            return not isinstance(c, int) or 0 <= c - lag < NBATCH

        def before(c, h, i):
            return c - 1, 1 - h, (i if h else i - 1)

        def bodies(eng, body, between=()):
            between = dict(between)
            body(0)
            at = 1
            for stop in [*sorted(between), NBODY]:
                if stop > at:
                    with eng.Fori(at, stop) as i:
                        body(i)
                at = stop
                if stop in between:
                    between[stop]()
            body(NBODY)

        def live(i, k, lag):
            return not isinstance(i, int) or 0 <= 8 * i + k - lag < NG

        class Order:

            def __init__(self, eng, s):
                self.eng, self.s, self.start, self.n = eng, s, 0, 0

            def link(self, ins):
                self.n += 1
                ins.then_inc(self.s, 1)
                self.eng.wait_ge(self.s, self.start + self.n)

            def rounds(self, body, slots):
                start = self.start + self.n

                def counted(c, h, i):
                    self.start, self.n = start + c, 0
                    body(c, h, i)
                    assert self.n == 1

                rounds(self.eng, counted, slots)
                self.start, self.n = start + NBATCH, 0

        STRIDE = 8
        at_step = [1 + STRIDE * (n + 1) for n in range(11)]
        parts = [0, 24, 48, 72, NTF]

        @block.sync
        def _(sp):
            def tiled(table, t0, t1):
                return table[t0 * P:t1 * P, :].rearrange("(t p) f -> p t f", p=P)

            def table_rows(table, c):
                return table[ds(c * (G * P), G * P), :].rearrange("(t p) f -> p t f", p=P)

            sp.dma_start(cnt_arrays[0], dst_halo).then_inc(S["counts_in_loaded"], 16)
            sp.dma_start(xq[:, 0:parts[1], :], tiled(x, 0, parts[1])).then_inc(s_x[0], 16)
            sp.dma_start(brow[:, :, :].rearrange("p k f -> p (k f)"), rows.partition_broadcast(P)).then_inc(S["weights_loaded"], 16)
            for n in range(1, 4):
                sp.dma_start(xq[:, parts[n]:parts[n + 1], :], tiled(x, parts[n], parts[n + 1])).then_inc(s_x[n], 16)
            sp.wait_ge(S["pad_zeroed"], 2)
            sp.dma_start(xq[0:NREST, NTF, :], x[NTF * P:N, :]).then_inc(s_x[3], 16)
            sp.dma_start(wmat[:, :, :], mats.rearrange("k p f -> p k f")).then_inc(S["weights_loaded"], 16)
            sp.dma_start(we_sb[0:DE, :], we).then_inc(S["weights_loaded"], 16)
            sp.dma_start(dloc[:, :].bitcast(I32), dst_tiles).then_inc(S["tile_arrays_loaded"], 16)
            sp.dma_start(coef[:, :].bitcast(I32), tile_base.partition_broadcast(P)).then_inc(S["tile_arrays_loaded"], 16)
            sp.dma_start(base[0:1, :], tile_base.rearrange("(a t) -> a t", a=1)).then_inc(S["tile_arrays_loaded"], 16)

            def store_p(c, h, i):
                if has(c):
                    sp.wait_ge(S["ht0_ready"], c + 1)
                    sp.dma_start(ht_rows[ds(c * P, P), :], ht0[h]).then_inc(S2["ht_stored"][h], 16)
                if has(c, 1):
                    c, h, i = before(c, h, i)
                    sp.wait_ge(S["p_ready"], c + 1)
                    sp.dma_start(table_rows(p_table, c), four(p_out[h])).then_inc(S2["p_stored"][h], 16)

            pairs(sp, store_p, lag=1)

            def store_scalars(n):
                sp.wait_ge(S["scalars_ready"], n + 1)
                tot = (cnt_arrays, soft_arrays)[n][3]
                sp.dma_start(coef_flat[n].rearrange("(p l) -> p l", p=P), tot).then_inc(S["scalars_stored"], 16)

            def stage_scalars(n):
                whole = T // P
                sp.wait_ge(S["scalars_stored"], 16 * n + 16)
                sp.dma_start(stage[:, 0:whole, :], coef_flat[n][0:whole * P * P].rearrange("(b t e) -> t b e", t=P, e=P)).then_inc(S["scalars_staged"], 16)
                sp.dma_start(stage[0:T - whole * P, whole, :], coef_flat[n][whole * P * P:EP].rearrange("(t e) -> t e", e=P)).then_inc(S["scalars_staged"], 16)

            def load_idx(layer, half, h, free):
                if free is not None:
                    sp.wait_ge(free, 4 * half - 4)
                sp.dma_start(idx[:, h, :], src_ring[ds(half, 1), :, :].rearrange("a p t -> (a p) t")).then_inc(s_idx[layer][h], 16)

            def loads0(i):
                for h in range(2):
                    half = 2 * i + h
                    if later(i):
                        load_idx(0, half, h, S["z_ready"])
                    for c in range(2):
                        chunk = 2 * half + c
                        if later(chunk, 2):
                            sp.wait_ge(S["z_in_psum"], 2 * chunk - 2)
                        sp.dma_start(ef_ring[0:DE, c * 1024:(c + 1) * 1024],
                                     edge_t[ds(chunk, 1), :, :].rearrange("a p t -> (a p) t")).then_inc(S2["edges_loaded"][c], 16)

            def load_soft():
                sp.wait_ge(S["coef_filled"], FILLS)
                sp.dma_start(soft_arrays[0], dst_halo).then_inc(S["soft_in_loaded"], 16)
                sp.dma_start(wgt, weight_flat.rearrange("(p l) -> p l", p=P)).then_inc(S["soft_in_loaded"], 16)

            def reload_x():
                sp.wait_ge(S["pad_zeroed"], 3)
                for n in range(4):
                    sp.dma_start(xq[:, parts[n]:parts[n + 1], :], tiled(x, parts[n], parts[n + 1])).then_inc(S["x_reloaded"], 16)
                sp.dma_start(xq[0:NREST, NTF, :], x[NTF * P:N, :]).then_inc(S["x_reloaded"], 16)

            for h in range(2):
                load_idx(0, h, h, None)
            store_scalars(0)
            stage_scalars(0)
            sp.wait_ge(S["ring_zeroed"], 1)
            loads0(0)
            at = 1
            for stop, what in ((2, load_soft), (at_step[-1] + 1, lambda: store_scalars(1)), (at_step[-1] + 5, reload_x), (NPOOL, None)):
                with sp.Fori(at, stop) as i:
                    loads0(i)
                at = stop
                if what:
                    what()

            def load_ht(c, h, i):
                if later(c, 4):
                    sp.wait_ge(S["x1_in_psum"], c - 3)
                elif h < 2:
                    sp.wait_ge(S["z_in_psum"], NG)
                else:
                    sp.wait_ge(S["m1t_in_psum"], NG)
                sp.dma_start(ht_in[h], ht_rows[ds(c * P, P), :]).then_inc(S2["ht_loaded"][h], 16)

            rounds(sp, load_ht, 4)
            sp.wait_ge(S["sums0_added"], T)
            stage_scalars(1)
            for h in range(2):
                load_idx(1, h, h, None)

            def store_h2(c, h, i):
                sp.wait_ge(S["h2_ready"], c + 1)
                sp.dma_start(table_rows(h_table, c), four(h2_out[h])).then_inc(S2["h2_stored"][h], 16)

            rounds(sp, store_h2, 4)
            for h in range(4):
                sp.wait_ge(S2["h2_stored"][h], 16 * used(4, h))

            def beside1(c, h, i):
                if has(c):
                    if later(c, 2):
                        sp.wait_ge(S["h2_turned"], c - 1)
                    sp.dma_start(four(h2_in[h]), table_rows(h_table, c)).then_inc(S2["h2_loaded"][h], 16)
                if has(c, 2):
                    sp.wait_ge(S["self_ready"], c - 1)
                    sp.dma_start(table_rows(self_rows, c - 2), four(self_out[h])).then_inc(S2["self_stored"][h], 16)
                if later(c):
                    for half in range(2):
                        load_idx(1, 2 * c + half, half, S["sums1_in_psum"])

            pairs(sp, beside1, lag=2)
            with sp.Fori(NBATCH + 2, NPOOL) as i:
                for h in range(2):
                    load_idx(1, 2 * i + h, h, S["sums1_in_psum"])

            for h in range(2):
                sp.wait_ge(S2["self_stored"][h], 16 * used(2, h))

            def load_self(c, h, i):
                if later(c, 4):
                    sp.wait_ge(S["u_ready"], c - 3)
                sp.dma_start(four(self_in[h]), table_rows(self_rows, c)).then_inc(S2["self_loaded"][h], 16)

            rounds(sp, load_self, 4)

            def store_out(c, h, i):
                sp.wait_ge(S["fin_ready"], c + 1)
                if isinstance(c, int) and (c + 1) * G > NTF:
                    for t in range(c * G, NTF):
                        sp.dma_start(out[t * P:(t + 1) * P, :], four(fin[h])[:, t - c * G, :]).then_inc(S2["out_stored"][h], 16)
                    sp.dma_start(out[NTF * P:N, :], four(fin[h])[0:NREST, NTF - c * G, :]).then_inc(S2["out_stored"][h], 16)
                else:
                    sp.dma_start(table_rows(out, c), four(fin[h])).then_inc(S2["out_stored"][h], 16)

            pairs(sp, store_out)
            extra = NTF - NTF // G * G
            for h in range(2):
                sp.wait_ge(S2["out_stored"][h], 16 * (used(2, h) + (extra if (NBATCH - 1) % 2 == h else 0)))

        @block.gpsimd
        def _(pool):
            pool.memset(xq[:, NTF:NT, :], 0.0).then_inc(S["pad_zeroed"], 1)
            pool.memset(we_sb[:, :], 0.0).then_inc(S["pad_zeroed"], 1)
            pool.memset(ident[:, :], 0.0).then_inc(S["pool_order"], 1)
            pool.iota(iota[:, :], [[1, P]], base=0, channel_multiplier=0,
                      allow_small_or_imprecise_dtypes=True).then_inc(S["constants_made"], 1)
            pool.memset(ones_b[:, :], 1.0).then_inc(S["constants_made"], 1)
            pool.memset(onec[:, :], 1.0).then_inc(S["constants_made"], 1)
            pool.memset(eps[:, :], LN_EPS).then_inc(S["constants_made"], 1)
            pool.memset(zeroc[:, :], 0.0).then_inc(S["constants_made"], 1)
            pool.wait_ge(S["pool_order"], 1)
            pool.affine_select(out=ident[:, :], in_=ident[:, :], compare_op=ALU.not_equal, fill=1.0,
                               base=0, pattern=[[-1, P]], channel_multiplier=1).then_inc(S["constants_made"], 1)
            pool.memset(ef_ring, 0.0).then_inc(S["ring_zeroed"], 1)

            def gather(layer, table, i):
                for h in range(2):
                    pool.wait_ge(s_idx[layer][h], 16 * i + 16)
                    pool.sem_inc(S["pool_turns"], 1)
                    for k in range(4):
                        for j in range(G):
                            pool.indirect_dma_start(
                                out=rows_ring[:, 16 * h + G * k + j, :], out_offset=None, in_=table[:, :],
                                in_offset=bass.IndirectOffsetOnAxis(ap=idx[:, h, G * k + j:G * k + j + 1], axis=0),
                            ).then_inc(s_rows[layer][4 * h + k], 16)

            pool.wait_ge(S["bias_ready"], 1)
            for h in range(2):
                pool.wait_ge(S2["p_stored"][h], 16 * used(2, h))
                pool.wait_ge(S2["ht_stored"][h], 16 * used(2, h))
            each(pool, NPOOL, lambda i: gather(0, p_table, i))

            with pool.Fori(0, NBATCH) as c:
                pool.wait_ge(S["x1_sums_copied"], c + 1)
                pool.sem_inc(S["pool_turns"], 1)
                pool.tensor_copy(acc[:, batch(c)], zeroc[:, :].to_broadcast([P, G * P])).then_inc(S["sums_zeroed1"], 1)
            for h in range(4):
                pool.wait_ge(S2["h2_stored"][h], 16 * used(4, h))
            each(pool, NPOOL, lambda i: gather(1, h_table, i))

            with pool.Fori(0, NBATCH) as c:
                pool.wait_ge(S["centred_ready"], c + 1)
                pool.sem_inc(S["pool_turns"], 1)
                u4 = four(acc[:, batch(c)])
                pool.tensor_tensor(u4, u4, over4("gamma"), ALU.mult).then_inc(S["scaled_ready"], 1)

        @block.scalar
        def _(act):
            act.wait_ge(S["constants_made"], 6)
            act.wait_ge(S["var0_ready"], 1)
            act.activation(sc_a[:, :], var[:, :], ACT.Sqrt, bias=eps[:, :]).then_inc(S["root0_ready"], 1)

            def table_p(c, h, i):
                if has(c):
                    act.wait_ge(S["normed0_turned"], c + 1)
                    if later(c, 2):
                        act.wait_ge(S["p_in_psum"], c - 1)
                        act.wait_ge(S2["ht_stored"][h], 16 * i)
                    act.activation(ht0[h], ps_z[h][:, :], ACT.Relu).then_inc(S["ht0_ready"], 1)
                if has(c, 1):
                    c, h, i = before(c, h, i)
                    act.wait_ge(S["p_in_psum"], c + 1)
                    if later(c, 2):
                        act.wait_ge(S2["p_stored"][h], 16 * i)
                    act.activation(p_out[h], ps_m1t[h][:, :], ACT.Copy).then_inc(S["p_ready"], 1)

            pairs(act, table_p, lag=1)

            def fill(n):
                for q in range(FILLS):
                    act.wait_ge(S["scalars_turned"], n * FILLS + q + 1)
                    width = min(512, T - 512 * q)
                    act.activation(coef[:, 512 * q:512 * q + width], ps_m1t[q % 2][:, 0:width], ACT.Copy).then_inc(S["coef_filled"], 1)

            act.wait_ge(S["counts_made"], 1)
            at0, at1 = 2 * LEN + 2, 3 * LEN + 2
            for a, b_ in ((0, at0), (at1, NP)):
                act.activation(acc[:, a:b_], zeroc[:, :].to_broadcast([P, b_ - a]), ACT.Copy).then_inc(S["sums_zeroed0"], 1)
            act.wait_ge(S["dloc_ready"], 1)
            act.wait_ge(S["scalars_stored"], 16)
            act.activation(acc[:, at0:at1], zeroc[:, :].to_broadcast([P, at1 - at0]), ACT.Copy).then_inc(S["sums_zeroed0"], 1)
            fill(0)

            def layer0(i):
                for k in range(8):
                    if live(i, k, 1):
                        g, slot = 8 * i + k - 1, (k + 1) % 2
                        act.wait_ge(S["m1t_in_psum"], g + 1)
                        if later(g, 2):
                            act.wait_ge(S["m2_in_psum"], g - 1)
                        act.activation(m1t_sb[slot], ps_m1t[slot][:, :], ACT.Relu).then_inc(S["m1t_ready"], 1)
                    if live(i, k, 2):
                        g, slot = 8 * i + k - 2, k % 2
                        act.wait_ge(S["m2_in_psum"], g + 1)
                        if later(g, 2):
                            act.wait_ge(S["sums0_in_psum"], g - 1)
                        act.activation(m2_sb[slot], ps_m2[slot][:, :], ACT.Relu).then_inc(S["m2_ready"], 1)

            def exponentials():
                act.wait_ge(S["less_max_ready"], 1)
                act.activation(wgt, wgt, ACT.Exp).then_inc(S["exp_ready"], 1)

            bodies(act, layer0, {at_step[4]: exponentials})

            def copy_sums(copied, read):
                def body(c, h, i):
                    if later(c, 2):
                        act.wait_ge(read, c - 1)
                    act.activation(sums_in[h], acc[:, batch(c)], ACT.Copy).then_inc(copied, 1)
                pairs(act, body)

            act.wait_ge(S["z_in_psum"], NG)
            act.wait_ge(S["sums0_added"], T)
            copy_sums(S["x1_sums_copied"], S["x1_in_psum"])
            fill(1)
            act.wait_ge(S["var1_ready"], 1)
            act.activation(sc_a[:, :], var[:, :], ACT.Sqrt, bias=eps[:, :]).then_inc(S["root1_ready"], 1)

            def table_h2(c, h, i):
                act.wait_ge(S["normed1_ready"], c + 1)
                if later(c, 4):
                    act.wait_ge(S2["h2_stored"][h], 16 * i)
                act.activation(h2_out[h], normed1[h % 2], ACT.Relu).then_inc(S["h2_ready"], 1)

            rounds(act, table_h2, 4)

            def self_part(c, h, i):
                act.wait_ge(S["h2_turned"], c + 1)
                if later(c, 2):
                    act.wait_ge(S["self_in_psum"], c - 1)
                act.activation(h2t[h], ps_m1t[h][:, :], ACT.Copy).then_inc(S["h2t_ready"], 1)
                act.wait_ge(S["self_in_psum"], c + 1)
                if later(c, 2):
                    act.wait_ge(S2["self_stored"][h], 16 * i)
                act.activation(self_out[h], ps_m2[h][:, :], ACT.Copy).then_inc(S["self_ready"], 1)

            pairs(act, self_part)

            act.wait_ge(S["sums1_added"], T)

            def norms(c, h, i):
                if later(c, 4):
                    act.wait_ge(S["norms_in_psum"], c - 3)
                act.activation(squares[h], acc[:, batch(c)], ACT.Square).then_inc(S["squares_ready"], 1)

            rounds(act, norms, 4)
            act.wait_ge(S["norms_in_psum"], NBATCH)
            act.activation(sc_a[:, :], ps_z[0][:, 0:NT], ACT.Sqrt).then_inc(S["norm_root_ready"], 1)
            copy_sums(S["nb_sums_copied"], S["nb_in_psum"])
            act.wait_ge(S["unit_arg_ready"], 1)
            act.activation(sc_b[:, :], sc_b[:, :], ACT.Sqrt).then_inc(S["unit_root_ready"], 1)
            act.wait_ge(S["var2_ready"], 1)
            act.activation(sc_a[:, :], sc_a[:, :], ACT.Sqrt, bias=eps[:, :]).then_inc(S["root2_ready"], 1)

        @block.vector
        def _(dve):
            order = Order(dve, S["vector_order"])
            link = order.link

            def row_stats(src, c):
                dve.sem_inc(S["vector_turns"], 1)
                for t in range(G):
                    ins = dve.bn_stats(flat(stat6[:, ds(c * G + t, 1), :]), src(c, t))
                return ins

            def mean_and_var():
                me, se, mo, so = (stat6[:, :, n] for n in (1, 2, 4, 5))
                link(dve.tensor_tensor(mean[:, :], me, mo, ALU.subtract))
                link(dve.tensor_tensor(mean[:, :], mean[:, :], mean[:, :], ALU.mult))
                link(dve.scalar_tensor_tensor(var[:, :], mean[:, :], P / 4.0, se, ALU.mult, ALU.add))
                link(dve.tensor_tensor(var[:, :], var[:, :], so, ALU.add))
                link(dve.tensor_scalar(var[:, :], var[:, :], 1.0 / P, None, ALU.mult))
                link(dve.tensor_tensor(mean[:, :], me, mo, ALU.add))
                link(dve.tensor_scalar(mean[:, :], mean[:, :], 0.5, None, ALU.mult))

            def normalise(dst, src, c, scale):
                for t in range(G):
                    ins = dve.tensor_scalar(dst(t), src(c, t), of_tile(mean, c, t), of_tile(scale, c, t), ALU.subtract, ALU.mult)
                return ins

            link(dve.memset(rowk[:, :], 0.0))
            dve.wait_ge(S["constants_made"], 6)

            carries = [0]

            def scan(dst, mask, data, op0, op1, initial, back):
                way = slice(None, None, -1) if back else slice(None)
                link(dve.tensor_tensor_scan(dst[:, way], mask[:, way], data[:, way], initial, op0, op1))

            def carried_scan(dst, mask, data, op0, op1, initial, back):
                scan(dst, mask, data, op0, op1, initial, back)
                carries[0] += 1
                n = carries[0]
                end = dst[:, 0:1] if back else dst[:, LEN - 1:LEN]
                link(dve.tensor_copy(keep[:, 2:3], end))
                dve.sem_inc(S["ends_ready"], 1)
                dve.wait_ge(S["ends_turned"], n)
                link(dve.tensor_copy(rowk[0:1, 0:2 * P], ps_z[0][0:1, 0:2 * P]))
                dve.sem_inc(S["ends_read"], 1)
                ends, flags = rowk[0:1, 0:P], rowk[0:1, P:2 * P]
                if op0 == ALU.min:
                    link(dve.tensor_scalar(flags, flags, 2.0, -1.0, ALU.mult, ALU.add))
                    link(dve.tensor_scalar(flags, flags, BIG, None, ALU.mult))
                if back:
                    link(dve.tensor_tensor_scan(rowk[0:1, 3 * P:4 * P - 1][:, ::-1], flags[:, 1:P][:, ::-1], ends[:, 1:P][:, ::-1], initial, op0, op1))
                else:
                    link(dve.tensor_tensor_scan(rowk[0:1, 2 * P + 1:3 * P], flags[:, 0:P - 1], ends[:, 0:P - 1], initial, op0, op1))
                dve.sem_inc(S["carry_ready"], 1)
                dve.wait_ge(S["carry_turned"], n)
                link(dve.tensor_copy(keep[:, 3:4], ps_z[1][:, 0:1]))
                dve.sem_inc(S["carry_read"], 1)
                scan(dst, mask, data, op0, op1, keep[:, 3:4], back)

            def equalities(arrays):
                halo, _, _, _, eq = arrays
                link(dve.tensor_tensor(eq, halo[:, 1:LEN + 2], halo[:, 0:LEN + 1], ALU.is_equal))

            def forward(arrays, mask, data, op0, op1, initial):
                carried_scan(arrays[2], mask, data, op0, op1, initial, False)

            def back_over(arrays):
                _, _, fwd, tot, eq = arrays
                same_after = eq[:, 1:LEN + 1]
                link(dve.scalar_tensor_tensor(fwd, same_after, 0.0, fwd, ALU.is_equal, ALU.mult))
                carried_scan(tot, same_after, fwd, ALU.mult, ALU.add, 0.0, True)

            link(dve.memset(keep[:, :], 0.0))
            dve.wait_ge(S["counts_in_loaded"], 16)
            equalities(cnt_arrays)
            cnt_eq = cnt_arrays[4]
            link(dve.tensor_reduce(keep[:, 0:1], cnt_eq[:, 0:LEN], AX.X, ALU.min))
            link(dve.tensor_reduce(keep[:, 1:2], cnt_eq[:, 1:LEN + 1], AX.X, ALU.min))
            forward(cnt_arrays, cnt_eq[:, 0:LEN], onec[:, :].to_broadcast([P, LEN]), ALU.mult, ALU.add, 0.0)
            back_over(cnt_arrays)
            dve.sem_inc(S["counts_made"], 1)

            for n in range(4):
                dve.wait_ge(s_x[n], 16 if n < 3 else 32)
                with dve.Fori(parts[n] // (3 * G), parts[n + 1] // (3 * G)) as c:
                    for third in range(3):
                        row_stats(q_tile, 3 * c + third)
            row_stats(q_tile, NBATCH - 1)
            link(dve.memset(keep[:, 2:3], 0.0))
            mean_and_var()
            dve.sem_inc(S["var0_ready"], 1)

            dve.wait_ge(S["weights_loaded"], 48)
            link(dve.tensor_tensor(b["b_self"], b["b_self"], b["b_nb"], ALU.add))
            biases, bias_parts = flat(brow[:, 0:4, :]), flat(bias3[:, :, :])
            link(dve.tensor_copy(split, biases))
            link(dve.tensor_scalar(bias_parts, split, ident[:, 0:1], None, ALU.mult))
            link(dve.tensor_tensor(rest, biases, split, ALU.subtract))
            for part in (1, 2):
                link(dve.tensor_copy(split, rest))
                link(dve.scalar_tensor_tensor(bias_parts, split, ident[:, part:part + 1], bias_parts, ALU.mult, ALU.add))
                if part == 1:
                    link(dve.tensor_tensor(rest, rest, split, ALU.subtract))
            dve.sem_inc(S["bias_ready"], 1)
            dve.wait_ge(S["root0_ready"], 1)
            link(dve.reciprocal(sc_a[:, :], sc_a[:, :]))

            def norm0(c, h, i):
                if later(c, 2):
                    dve.wait_ge(S["normed0_turned"], c - 1)
                normalise(lambda t: normed0[h][:, t, :], q_tile, c, sc_a).then_inc(S["normed0_ready"], 1)

            pairs(dve, norm0)
            dve.reciprocal(cnt_arrays[3], cnt_arrays[3]).then_inc(S["scalars_ready"], 1)

            dve.wait_ge(S["tile_arrays_loaded"], 48)
            dve.tensor_tensor(dloc[:, :], dloc[:, :].bitcast(I32), coef[:, :].bitcast(I32), ALU.subtract).then_inc(S["dloc_ready"], 1)

            _, lim, fwd, tot, eq = soft_arrays
            same_before = eq[:, 0:LEN]

            def limits():
                dve.wait_ge(S["soft_in_loaded"], 32)
                equalities(soft_arrays)
                link(dve.tensor_scalar(lim, same_before, 2.0, -1.0, ALU.mult, ALU.add))
                link(dve.tensor_scalar(lim, lim, BIG, None, ALU.mult))

            def less_max():
                dve.tensor_tensor(wgt, wgt, tot, ALU.subtract).then_inc(S["less_max_ready"], 1)

            def forward_sums():
                dve.wait_ge(S["exp_ready"], 1)
                forward(soft_arrays, same_before, wgt, ALU.mult, ALU.add, 0.0)

            def invert(n):
                part = tot[:, n * LEN // 4:(n + 1) * LEN // 4]
                link(dve.reciprocal(part, part))
                if n == 3:
                    dve.tensor_tensor(tot, tot, wgt, ALU.mult).then_inc(S["scalars_ready"], 1)

            def clear_last_tiles():
                dve.wait_ge(S["scalars_stored"], 32)
                dve.memset(xq[:, NTF:NT, :], 0.0).then_inc(S["pad_zeroed"], 1)

            steps = [limits,
                     lambda: forward(soft_arrays, lim, wgt, ALU.min, ALU.max, -BIG),
                     lambda: back_over(soft_arrays),
                     less_max,
                     lambda: None,
                     forward_sums,
                     lambda: back_over(soft_arrays),
                     lambda: invert(0), lambda: invert(1), lambda: invert(2), lambda: invert(3)]

            def bases(group):
                _, at = nc.values_load_multi_w_load_instructions(
                    base[0:1, ds(G * group, G)], engines=[mybir.EngineType.DVE], min_val=0, max_val=N,
                    skip_runtime_bounds_check_because="destinations are nodes or N")
                return at

            def sums_and_onehots(i, k, lag_sum, lag_hot, in_psum, added, hot):
                adds, hots = live(i, k, lag_sum), live(i, k, lag_hot)
                gs, gh = 8 * i + k - lag_sum, 8 * i + k - lag_hot
                if adds:
                    at = bases(gs)
                    dve.wait_ge(in_psum, gs + 1)
                for j in range(G):
                    if adds:
                        if later(gs * G + j):
                            dve.wait_ge(added, gs * G + j)
                        win = acc[:, ds(at[j], P)]
                        dve.tensor_tensor(win, win, ps_agg[k % 2][:, j * P:(j + 1) * P], ALU.add).then_inc(added, 1)
                    if hots:
                        t = gh * G + j
                        ins = dve.tensor_scalar(onehot[:, k % 2, j * P:(j + 1) * P], iota[:, :], dloc[:, ds(t, 1)], coef[:, ds(t, 1)],
                                                ALU.is_equal, ALU.mult)
                if hots:
                    ins.then_inc(hot, 1)

            def layer0(i):
                for k in range(8):
                    g, slot = 8 * i + k, k % 2
                    if live(i, k, 0):
                        dve.wait_ge(S["z_in_psum"], g + 1)
                        dve.wait_ge(s_rows[0][k], 64 * i + 64)
                        if later(g, 2):
                            dve.wait_ge(S["m1t_in_psum"], g - 1)
                        dve.tensor_tensor(four(z_sb[slot]), four(ps_z[slot][:, :]),
                                          rows_ring[:, G * k:G * k + G, :], ALU.add).then_inc(S["z_ready"], 1)
                    sums_and_onehots(i, k, 4, 2, S["sums0_in_psum"], S["sums0_added"], S["onehot0_ready"])

            dve.wait_ge(S["coef_filled"], FILLS)
            dve.wait_ge(S["sums_zeroed0"], 3)
            bodies(dve, layer0, [*zip(at_step, steps), (at_step[-1] + 3, clear_last_tiles)])

            dve.wait_ge(S["x_reloaded"], 80)

            def x1(c, h, i):
                dve.wait_ge(S["x1_in_psum"], c + 1)
                ins = dve.tensor_tensor(q_rows(c), q_rows(c), four(ps_z[h][:, :]), ALU.add)
                link(ins)
                dve.sem_inc(S["x1_added"], 1)
                row_stats(q_tile, c)

            order.rounds(x1, 2)
            link(dve.memset(keep[:, 2:3], 0.0))
            mean_and_var()
            dve.sem_inc(S["var1_ready"], 1)
            dve.wait_ge(S["root1_ready"], 1)
            link(dve.reciprocal(sc_a[:, :], sc_a[:, :]))

            def norm1(c, h, i):
                if later(c, 2):
                    dve.wait_ge(S["h2_ready"], c - 1)
                normalise(lambda t: four(normed1[h])[:, t, :], q_tile, c, sc_a).then_inc(S["normed1_ready"], 1)

            pairs(dve, norm1)

            def layer1(i):
                for k in range(8):
                    sums_and_onehots(i, k, 2, 0, S["sums1_in_psum"], S["sums1_added"], S["onehot1_ready"])

            dve.wait_ge(S["coef_filled"], 2 * FILLS)
            dve.wait_ge(S["sums_zeroed1"], NBATCH)
            dve.sem_inc(S["vector_turns"], 1)

            def beside1(i):
                layer1(i)
                dve.tensor_tensor(q_rows(i), q_rows(i), over4("beta"), ALU.add)

            each(dve, NBATCH, beside1)
            with dve.Fori(NBATCH, NBODY) as i:
                layer1(i)
            layer1(NBODY)

            dve.wait_ge(S["norm_root_ready"], 1)
            link(dve.tensor_scalar(sc_a[:, :], sc_a[:, :], NORM_EPS, None, ALU.add))
            link(dve.reciprocal(sc_a[:, :], sc_a[:, :]))

            def u_rows(c, h, i):
                if has(c):
                    dve.wait_ge(S["nb_in_psum"], c + 1)
                    dve.wait_ge(S2["self_loaded"][h], 16 * i + 16)
                for t in range(G) if has(c) else ():
                    ins = dve.scalar_tensor_tensor(u_tile(c, t), ps_nb[h][:, t * P:(t + 1) * P], of_tile(sc_a, c, t),
                                                   four(self_in[h])[:, t, :], ALU.mult, ALU.add)
                if has(c):
                    ins.then_inc(S["u_ready"], 1)
                if has(c, 1):
                    dve.wait_ge(S["u_ready"], c)
                    row_stats(u_tile, c - 1)

            rounds(dve, u_rows, 4, lag=1)
            link(dve.memset(keep[:, 2:3], 0.0))
            mean_and_var()
            link(dve.tensor_tensor(sc_b[:, :], mean[:, :], mean[:, :], ALU.mult))
            link(dve.tensor_tensor(sc_b[:, :], sc_b[:, :], var[:, :], ALU.add))
            dve.tensor_scalar(sc_b[:, :], sc_b[:, :], P / 4.0, None, ALU.mult).then_inc(S["unit_arg_ready"], 1)
            dve.wait_ge(S["unit_root_ready"], 1)
            link(dve.tensor_scalar(sc_b[:, :], sc_b[:, :], NORM_EPS, None, ALU.add))
            link(dve.reciprocal(sc_b[:, :], sc_b[:, :]))
            link(dve.tensor_scalar(sc_b[:, :], sc_b[:, :], 0.5, None, ALU.mult))
            link(dve.tensor_tensor(sc_a[:, :], sc_b[:, :], sc_b[:, :], ALU.mult))
            dve.tensor_tensor(sc_a[:, :], sc_a[:, :], var[:, :], ALU.mult).then_inc(S["var2_ready"], 1)
            dve.wait_ge(S["root2_ready"], 1)
            link(dve.reciprocal(sc_a[:, :], sc_a[:, :]))
            link(dve.tensor_tensor(sc_a[:, :], sc_a[:, :], sc_b[:, :], ALU.mult))

            def last(c, h, i):
                if has(c):
                    normalise(lambda t: u_tile(c, t), u_tile, c, sc_a).then_inc(S["centred_ready"], 1)
                if has(c, 2):
                    dve.wait_ge(S["scaled_ready"], c - 1)
                    if later(c, 4):
                        dve.wait_ge(S2["out_stored"][h], 16 * (i - 1))
                    dve.tensor_tensor(four(fin[h]), four(acc[:, batch(c - 2)]), q_rows(c - 2), ALU.add).then_inc(S["fin_ready"], 1)

            last(0, 0, 0)
            last(1, 1, 0)
            last(2, 0, 1)
            last(3, 1, 1)
            with dve.Fori(2, NBATCH // 2) as i:
                for h in range(2):
                    last(2 * i + h, h, i)
            for c in range(NBATCH // 2 * 2, NBATCH + 2):
                last(c, c % 2, c // 2)

        @block.tensor
        def _(pe):
            def turn(dst, src):
                for d, s in zip(tiles(dst), src):
                    ins = pe.transpose(d, s, ident[:, :])
                return ins

            def products(dst, pairs_of, bias=None):
                if bias is not None:
                    pe.matmul(four(dst), ones_b[:, :], bias_rows(bias), start=True, stop=False)
                for t in range(G):
                    for n, (left, right) in enumerate(pairs_of):
                        ins = pe.matmul(tiles(dst)[t], left[t], right[t] if isinstance(right, list) else right,
                                        start=bias is None and n == 0,
                                        stop=n == len(pairs_of) - 1 and (bias is None or t == G - 1))
                return ins

            def carry(n, back, groups):
                if groups:
                    pe.wait_ge(S["z_ready"], groups)
                pe.wait_ge(S["ends_ready"], n)
                pe.matmul(ps_z[0][0:1, 0:P], keep[:, 2:3], ident[:, :], start=True, stop=True)
                pe.matmul(ps_z[0][0:1, P:2 * P], keep[:, back:back + 1], ident[:, :], start=True, stop=True).then_inc(S["ends_turned"], 1)
                pe.wait_ge(S["carry_ready"], n)
                at = (3 if back else 2) * P
                pe.matmul(ps_z[1][:, 0:1], rowk[0:1, at:at + P], onec[0:1, 0:1], start=True, stop=True).then_inc(S["carry_turned"], 1)
                pe.wait_ge(S["ends_read"], n)
                pe.wait_ge(S["carry_read"], n)

            pe.wait_ge(S["constants_made"], 6)
            carry(1, 0, 0)
            carry(2, 1, 0)

            pe.wait_ge(S["weights_loaded"], 48)
            pe.wait_ge(S["bias_ready"], 1)

            def table_p(c, h, i):
                if has(c):
                    pe.wait_ge(S["normed0_ready"], c + 1)
                    if later(c, 2):
                        pe.wait_ge(S["ht0_ready"], c - 1)
                    turn(ps_z[h][:, :], [normed0[h][:, t, :] for t in range(G)]).then_inc(S["normed0_turned"], 1)
                if has(c, 1):
                    c, h, i = before(c, h, i)
                    pe.wait_ge(S["ht0_ready"], c + 1)
                    if later(c, 2):
                        pe.wait_ge(S["p_ready"], c - 1)
                    products(ps_m1t[h][:, :], [(tiles(ht0[h]), w["wn"])], "b_msg").then_inc(S["p_in_psum"], 1)

            pairs(pe, table_p, lag=1)

            def fill(n):
                pe.wait_ge(S["scalars_staged"], 32 * n + 32)
                for q in range(FILLS):
                    if n * FILLS + q > 1:
                        pe.wait_ge(S["coef_filled"], n * FILLS + q - 1)
                    for j in range(4 * q, min(4 * q + 4, T // P + 1)):
                        h = min(P, T - j * P)
                        ins = pe.transpose(ps_m1t[q % 2][:, (j % 4) * P:(j % 4) * P + h], stage[0:h, j, :], ident[0:h, 0:h])
                    ins.then_inc(S["scalars_turned"], 1)

            fill(0)
            pe.wait_ge(S["coef_filled"], FILLS)

            def layer0(i):
                for k in range(8):
                    if live(i, k, 0):
                        g, slot, c = 8 * i + k, k % 2, k // 2 % 2
                        pe.wait_ge(S2["edges_loaded"][c], 32 * i + 16 * (k // 4) + 16)
                        if later(g, 2):
                            pe.wait_ge(S["z_ready"], g - 1)
                        at = c * 1024 + slot * 512
                        products(ps_z[slot][:, :], [(tiles(ef_ring[:, at:at + 512]), we_sb[:, :])]).then_inc(S["z_in_psum"], 1)
                    if live(i, k, 1):
                        g, slot = 8 * i + k - 1, (k + 1) % 2
                        pe.wait_ge(S["z_ready"], g + 1)
                        if later(g, 2):
                            pe.wait_ge(S["m1t_ready"], g - 1)
                        turn(ps_m1t[slot][:, :], tiles(z_sb[slot])).then_inc(S["m1t_in_psum"], 1)
                    if live(i, k, 2):
                        g, slot = 8 * i + k - 2, k % 2
                        pe.wait_ge(S["m1t_ready"], g + 1)
                        if later(g, 2):
                            pe.wait_ge(S["m2_ready"], g - 1)
                        products(ps_m2[slot][:, :], [(tiles(m1t_sb[slot]), w["w2"])], "b2").then_inc(S["m2_in_psum"], 1)
                    if live(i, k, 3):
                        g, slot = 8 * i + k - 3, (k + 1) % 2
                        pe.wait_ge(S["m2_ready"], g + 1)
                        pe.wait_ge(S["onehot0_ready"], g + 1)
                        if later(g, 2):
                            pe.wait_ge(S["sums0_added"], 4 * g - 4)
                        products(ps_agg[slot][:, :], [(tiles(m2_sb[slot]), tiles(onehot[:, slot, :]))]).then_inc(S["sums0_in_psum"], 1)

            between = {}
            for n, (step, back) in enumerate(((1, 0), (2, 1), (5, 0), (6, 1))):
                between[at_step[step]] = lambda n=n, back=back, step=step: carry(3 + n, back, 8 * at_step[step])
            bodies(pe, layer0, between)

            def x1(c, h, i):
                pe.wait_ge(S2["ht_loaded"][h], 16 * i + 16)
                pe.wait_ge(S["x1_sums_copied"], c + 1)
                if later(c, 2):
                    pe.wait_ge(S["x1_added"], c - 1)
                products(ps_z[h % 2][:, :], [(tiles(ht_in[h]), w["wa1"]), (tiles(sums_in[h % 2]), w["wa2"])], "b_apply").then_inc(S["x1_in_psum"], 1)

            rounds(pe, x1, 4)
            fill(1)
            pe.wait_ge(S["coef_filled"], 2 * FILLS)

            def layer1(i):
                for k in range(8):
                    if live(i, k, 0):
                        g, slot = 8 * i + k, k % 2
                        pe.wait_ge(s_rows[1][k], 64 * i + 64)
                        pe.wait_ge(S["onehot1_ready"], g + 1)
                        if later(g, 2):
                            pe.wait_ge(S["sums1_added"], 4 * g - 4)
                        products(ps_agg[slot][:, :], [([rows_ring[:, G * k + j, :] for j in range(G)], tiles(onehot[:, slot, :]))]).then_inc(S["sums1_in_psum"], 1)

            def beside1(c, h, i):
                pe.wait_ge(S2["h2_loaded"][h], 16 * i + 16)
                if later(c, 2):
                    pe.wait_ge(S["h2t_ready"], c - 1)
                turn(ps_m1t[h][:, :], tiles(h2_in[h])).then_inc(S["h2_turned"], 1)
                layer1(c)
                pe.wait_ge(S["h2t_ready"], c + 1)
                if later(c, 2):
                    pe.wait_ge(S["self_ready"], c - 1)
                products(ps_m2[h][:, :], [(tiles(h2t[h]), w["wself"])], "b_sn").then_inc(S["self_in_psum"], 1)

            pairs(pe, beside1)
            with pe.Fori(NBATCH, NBODY) as i:
                layer1(i)

            def norms(c, h, i):
                pe.wait_ge(S["squares_ready"], c + 1)
                for t in range(G):
                    ins = pe.matmul(ps_z[0][:, ds(c * G + t, 1)], squares[h][:, t * P:(t + 1) * P], onec[:, :], start=True, stop=True)
                ins.then_inc(S["norms_in_psum"], 1)

            rounds(pe, norms, 4)

            def neighbours(c, h, i):
                pe.wait_ge(S["nb_sums_copied"], c + 1)
                if later(c, 4):
                    pe.wait_ge(S["u_ready"], c - 3)
                products(ps_nb[h][:, :], [(tiles(sums_in[h % 2]), w["wnb"])]).then_inc(S["nb_in_psum"], 1)

            rounds(pe, neighbours, 4)


_ARGS = ["x", "edge_t", "src_ring", "dst_halo", "dst_tiles", "tile_base", "weight_flat", "mats", "we", "rows"]


def kernel(x, src, dst, edge_attr_64, edge_weight, L0_gnn_W_msg_w, L0_gnn_W_msg_b, L0_gnn_W_msg2_w, L0_gnn_W_msg2_b,
           L0_gnn_W_apply_w, L0_gnn_W_apply_b, L1_gnn_W_self, L1_gnn_b_self, L1_gnn_W_nb, L1_gnn_b_nb, L1_gnn_gamma,
           L1_gnn_beta):
    import numpy as np
    import concourse.bacc as bacc
    from concourse.bass_utils import run_bass_kernel_spmd as run

    c = np.ascontiguousarray
    pad = EP - E
    dst_pad = np.pad(np.asarray(dst), (0, pad), constant_values=N)
    src_pad = np.pad(np.asarray(src), (0, pad))
    ends = np.pad(dst_pad, 1, constant_values=-1)
    edges = np.pad(np.asarray(edge_attr_64), ((0, pad), (0, 0)))
    wm, wa = np.asarray(L0_gnn_W_msg_w), np.asarray(L0_gnn_W_apply_w)
    arrays = {
        "x": c(x),
        "edge_t": c(edges.reshape(EP // 1024, 1024, DE).transpose(0, 2, 1)),
        "src_ring": c(src_pad.reshape(T // 16, 16, P).transpose(0, 2, 1)),
        "dst_halo": np.stack([ends[p * LEN:p * LEN + LEN + 2] for p in range(P)]),
        "dst_tiles": c(dst_pad.reshape(T, P).T),
        "tile_base": c(dst_pad.reshape(T, P)[:, 0]),
        "weight_flat": np.pad(np.asarray(edge_weight), (0, pad)),
        "mats": np.stack([wm[:, :P].T, wa[:, :P].T, np.asarray(L0_gnn_W_msg2_w).T, wa[:, P:].T,
                          np.asarray(L1_gnn_W_self), np.asarray(L1_gnn_W_nb)]),
        "we": c(wm[:, P:].T),
        "rows": np.concatenate([np.asarray(v) for v in (L0_gnn_W_msg_b, L0_gnn_W_msg2_b, L0_gnn_W_apply_b, L1_gnn_b_self,
                                                        L1_gnn_b_nb, L1_gnn_gamma, L1_gnn_beta)]),
    }
    nc = bacc.Bacc("TRN2", target_bir_lowering=False, num_devices=1)
    ins = [nc.dram_tensor(f"in_{n}", arrays[n].shape, mybir.dt.from_np(arrays[n].dtype), kind="ExternalInput").ap() for n in _ARGS]
    out = nc.dram_tensor("rows_out", (N, P), F32, kind="ExternalOutput").ap()
    gnn(nc, *ins, out)
    r = run(nc, [{f"in_{n}": arrays[n] for n in _ARGS}], core_ids=[0])
    return r.results[0]["rows_out"]
```
